# Optimizing a Trainium2 kernel written in Bass

```python
import numpy as np
import jax
import jax.numpy as jnp

def _softmax(x, axis=-1):
    return jax.nn.softmax(x, axis=axis)
def _gelu(x):
    return jax.nn.gelu(x, approximate=True)
def _silu(x):
    return jax.nn.silu(x)
def _sigmoid(x):
    return jax.nn.sigmoid(x)
def _layernorm(x, axis=-1, eps=1e-5):
    m = jnp.mean(x, axis=axis, keepdims=True)
    v = jnp.var(x, axis=axis, keepdims=True)
    return (x - m) / jnp.sqrt(v + eps)
def _scatter_add(tgt, idx, src, axis=0):
    return tgt.at[idx].add(src)
def _segment_sum(src, seg, n):
    return jax.ops.segment_sum(src, seg, n)

kernel_name = 'mk_adj_ffn_d4_adj_256_5ec9c3'

def setup_inputs(seed: int = 0):
    np.random.seed(seed)
    _w = jnp.asarray
    def _rec_inputs():
        import jax
        import jax.numpy as jnp
        _gk = jax.random.key(seed)
        x = -0.001547 + 1.001 * jax.random.normal(jax.random.fold_in(_gk, 1), (1024, 256), jnp.float32)
        _a = jax.random.bernoulli(jax.random.fold_in(_gk, 2), 0.03125, (1024, 1024))
        _a = jnp.logical_or(_a, jnp.swapaxes(_a, -1, -2))
        _a = jnp.logical_or(_a, jnp.eye(1024, dtype=bool))
        adj = _a.astype(jnp.int32)
        return x, adj
    x, adj = _rec_inputs()
    def _L0_gnn_setup():
        import jax, jax.numpy as jnp
        import numpy as np
        N_NODES = 1024
        IN_DIM = 256
        EDGE_DIM = 32
        HID = 32
        OUT_DIM = 128
        N_EDGE_EMB = 100000
        key = jax.random.key(seed)
        ks = jax.random.split(key, 16)
        g = lambda k, s, sc=0.05: jax.random.normal(k, s, jnp.float32) * sc
        z = lambda n: jnp.zeros((n,), jnp.float32)
        return {'x': g(ks[0], (N_NODES, IN_DIM), 1.0), 'neigh': g(ks[1], (N_NODES, IN_DIM), 1.0), 'edge_emb': g(ks[2], (N_EDGE_EMB, EDGE_DIM), 1.0), 'adj': jax.random.randint(ks[3], (N_NODES, N_NODES), 0, N_EDGE_EMB), 'Wx1': g(ks[4], (IN_DIM, HID)), 'bx1': z(HID), 'Wx2': g(ks[5], (HID, HID)), 'bx2': z(HID), 'Wn1': g(ks[6], (IN_DIM, HID)), 'bn1': z(HID), 'Wn2': g(ks[7], (HID, HID)), 'bn2': z(HID), 'We': g(ks[8], (EDGE_DIM, HID)), 'be': z(HID), 'Wv': g(ks[9], (IN_DIM, OUT_DIM)), 'bv': z(OUT_DIM), 'Wfe': g(ks[10], (EDGE_DIM, OUT_DIM)), 'bfe': z(OUT_DIM), 'Wfx': g(ks[11], (IN_DIM, OUT_DIM)), 'bfx': z(OUT_DIM)}
    _L0_gnn_all = _L0_gnn_setup()
    _L0_gnn_in = {k: v for k, v in _L0_gnn_all.items() if k in ('neigh', 'edge_emb', 'Wx1', 'bx1', 'Wx2', 'bx2', 'Wn1', 'bn1', 'Wn2', 'bn2', 'We', 'be', 'Wv', 'bv', 'Wfe', 'bfe', 'Wfx', 'bfx', )}
    del _L0_gnn_all

    def _L0_ffn_setup():
        import jax, jax.numpy as jnp
        import numpy as np
        B, S, H, F, E, K = (8, 4096, 256, 512, 16, 2)
        EPS = 1e-05
        key = jax.random.key(seed)
        ks = jax.random.split(key, 9)
        sc = 0.02
        return {'x': jax.random.normal(ks[0], (B, S, H), dtype=jnp.float32), 'gate_w': jax.random.normal(ks[1], (H, E), dtype=jnp.float32) * sc, 'gate_b': jnp.zeros((E,), dtype=jnp.float32), 'w1': jax.random.normal(ks[2], (E, H, F), dtype=jnp.float32) * sc, 'b1': jnp.zeros((E, F), dtype=jnp.float32), 'w2': jax.random.normal(ks[3], (E, F, H), dtype=jnp.float32) * sc, 'b2': jnp.zeros((E, H), dtype=jnp.float32), 'gamma': jnp.ones((H,), dtype=jnp.float32), 'beta': jnp.zeros((H,), dtype=jnp.float32)}
    _L0_ffn_all = _L0_ffn_setup()
    _L0_ffn_in = {k: v for k, v in _L0_ffn_all.items() if k in ('gate_w', 'gate_b', 'w1', 'b1', 'w2', 'b2', 'gamma', 'beta', )}
    del _L0_ffn_all

    def _L1_gnn_setup():
        import jax, jax.numpy as jnp
        import numpy as np
        N, IN_DIM, HEADS, OUT_DIM = (6144, 256, 4, 64)
        key = jax.random.key(seed)
        k_x, k_adj, k_w, k_as, k_ad = jax.random.split(key, 5)
        x = jax.random.normal(k_x, (N, IN_DIM), dtype=jnp.float32)
        adj = jax.random.randint(k_adj, (N, N), 0, 2, dtype=jnp.int32)
        idx = jnp.arange(N)
        adj = adj.at[idx, idx].set(1)
        lim_w = float(np.sqrt(1.0 / IN_DIM))
        W = jax.random.uniform(k_w, (HEADS * OUT_DIM, IN_DIM), minval=-lim_w, maxval=lim_w, dtype=jnp.float32)
        lim_a = float(np.sqrt(6.0 / (HEADS + OUT_DIM)))
        a_src = jax.random.uniform(k_as, (HEADS, OUT_DIM), minval=-lim_a, maxval=lim_a, dtype=jnp.float32)
        a_dst = jax.random.uniform(k_ad, (HEADS, OUT_DIM), minval=-lim_a, maxval=lim_a, dtype=jnp.float32)
        return {'x': x, 'adj': adj, 'W': W, 'a_src': a_src, 'a_dst': a_dst}
    _L1_gnn_all = _L1_gnn_setup()
    _L1_gnn_in = {k: v for k, v in _L1_gnn_all.items() if k in ('W', 'a_src', 'a_dst', )}
    del _L1_gnn_all

    def _L1_ffn_setup():
        import jax, jax.numpy as jnp
        import numpy as np
        B, T, D, H, E = (16, 4096, 256, 512, 8)
        key = jax.random.key(seed)
        ks = jax.random.split(key, 5)
        x = jax.random.normal(ks[0], (B, T, D), dtype=jnp.float32)
        gate_w = jax.random.normal(ks[1], (D, E), dtype=jnp.float32) * 0.02
        gate_b = jnp.zeros((E,), dtype=jnp.float32)
        W1 = jax.random.normal(ks[2], (E, D, H), dtype=jnp.float32) * 0.02
        b1 = jnp.zeros((E, H), dtype=jnp.float32)
        W2 = jax.random.normal(ks[3], (E, H, D), dtype=jnp.float32) * 0.02
        b2 = jnp.zeros((E, D), dtype=jnp.float32)
        return {'x': x, 'gate_w': gate_w, 'gate_b': gate_b, 'W1': W1, 'b1': b1, 'W2': W2, 'b2': b2}
    _L1_ffn_all = _L1_ffn_setup()
    _L1_ffn_in = {k: v for k, v in _L1_ffn_all.items() if k in ('gate_w', 'gate_b', 'W1', 'b1', 'W2', 'b2', )}
    del _L1_ffn_all

    def _L2_gnn_setup():
        import jax, jax.numpy as jnp
        import numpy as np
        N = 8192
        IN_F = 256
        OUT_F = 256
        key = jax.random.key(seed)
        k_v, k_adj, k1, k2, k3, kb = jax.random.split(key, 6)
        stdv = 1.0 / np.sqrt(OUT_F)
        V = jax.random.normal(k_v, (N, IN_F), dtype=jnp.float32)
        adj = jax.random.randint(k_adj, (N, N), 0, 4, dtype=jnp.int32)
        w1 = jax.random.uniform(k1, (IN_F, OUT_F), jnp.float32, -stdv, stdv)
        w2 = jax.random.uniform(k2, (IN_F, OUT_F), jnp.float32, -stdv, stdv)
        w3 = jax.random.uniform(k3, (IN_F, OUT_F), jnp.float32, -stdv, stdv)
        bias = jax.random.uniform(kb, (OUT_F,), jnp.float32, -stdv, stdv)
        return {'V': V, 'adj': adj, 'w1': w1, 'w2': w2, 'w3': w3, 'bias': bias}
    _L2_gnn_all = _L2_gnn_setup()
    _L2_gnn_in = {k: v for k, v in _L2_gnn_all.items() if k in ('w1', 'w2', 'w3', 'bias', )}
    del _L2_gnn_all

    def _L2_ffn_setup():
        import jax, jax.numpy as jnp
        import numpy as np
        B, S, D, F, E, K = (8, 2048, 256, 1024, 8, 2)
        key = jax.random.key(seed)
        ks = jax.random.split(key, 10)
        s = 0.02
        return {'x': jax.random.normal(ks[0], (B, S, D), dtype=jnp.float32), 'Wr': jax.random.normal(ks[1], (D, E), dtype=jnp.float32) * s, 'W1s': jax.random.normal(ks[2], (D, F), dtype=jnp.float32) * s, 'b1s': jnp.zeros((F,), dtype=jnp.float32), 'W2s': jax.random.normal(ks[3], (F, D), dtype=jnp.float32) * s, 'b2s': jnp.zeros((D,), dtype=jnp.float32), 'W1p': jax.random.normal(ks[4], (E, D, F), dtype=jnp.float32) * s, 'b1p': jnp.zeros((E, F), dtype=jnp.float32), 'W2p': jax.random.normal(ks[5], (E, F, D), dtype=jnp.float32) * s, 'b2p': jnp.zeros((E, D), dtype=jnp.float32)}
    _L2_ffn_all = _L2_ffn_setup()
    _L2_ffn_in = {k: v for k, v in _L2_ffn_all.items() if k in ('Wr', 'W1s', 'b1s', 'W2s', 'b2s', 'W1p', 'b1p', 'W2p', 'b2p', )}
    del _L2_ffn_all

    def _L3_gnn_setup():
        import jax, jax.numpy as jnp
        import numpy as np
        N = 8192
        IN_F = 256
        OUT_F = 256
        ALPHA = 0.2
        NEG_INF = -1000000000000.0
        key = jax.random.key(seed)
        k1, k2, k3, k4, k5 = jax.random.split(key, 5)
        inp = jax.random.normal(k1, (N, IN_F), dtype=jnp.float32)
        adj = jax.random.randint(k2, (N, N), 0, 2, dtype=jnp.int32)

        def xavier(k, shape, gain=1.414):
            fan_in, fan_out = (shape[0], shape[1])
            bound = gain * np.sqrt(6.0 / (fan_in + fan_out))
            return jax.random.uniform(k, shape, jnp.float32, -bound, bound)
        W = xavier(k3, (IN_F, OUT_F))
        a = xavier(k4, (2 * OUT_F, 1))
        wtrans = xavier(k5, (2 * IN_F, OUT_F))
        return {'inp': inp, 'adj': adj, 'W': W, 'a': a, 'wtrans': wtrans}
    _L3_gnn_all = _L3_gnn_setup()
    _L3_gnn_in = {k: v for k, v in _L3_gnn_all.items() if k in ('W', 'a', 'wtrans', )}
    del _L3_gnn_all

    def _L3_ffn_setup():
        import jax, jax.numpy as jnp
        import numpy as np
        D_MODEL = 256
        N_EXPERTS = 16
        HIDDEN = 512
        SCALE = 0.02
        key = jax.random.key(seed)
        ks = jax.random.split(key, 5)
        x = jax.random.normal(ks[0], (4, 8192, D_MODEL), dtype=jnp.float32)
        gate_w = jax.random.normal(ks[1], (D_MODEL, N_EXPERTS), dtype=jnp.float32) * SCALE
        gate_b = jnp.zeros((N_EXPERTS,), dtype=jnp.float32)
        w1 = jax.random.normal(ks[2], (N_EXPERTS, D_MODEL, HIDDEN), dtype=jnp.float32) * SCALE
        w2 = jax.random.normal(ks[3], (N_EXPERTS, D_MODEL, HIDDEN), dtype=jnp.float32) * SCALE
        w3 = jax.random.normal(ks[4], (N_EXPERTS, HIDDEN, D_MODEL), dtype=jnp.float32) * SCALE
        return {'x': x, 'gate_w': gate_w, 'gate_b': gate_b, 'w1': w1, 'w2': w2, 'w3': w3}
    _L3_ffn_all = _L3_ffn_setup()
    _L3_ffn_in = {k: v for k, v in _L3_ffn_all.items() if k in ('gate_w', 'gate_b', 'w1', 'w2', 'w3', )}
    del _L3_ffn_all

    return {
        "x": x,
        "adj": adj,
        "L0_gnn_neigh": _L0_gnn_in["neigh"],
        "L0_gnn_edge_emb": _L0_gnn_in["edge_emb"],
        "L0_gnn_Wx1": _L0_gnn_in["Wx1"],
        "L0_gnn_bx1": _L0_gnn_in["bx1"],
        "L0_gnn_Wx2": _L0_gnn_in["Wx2"],
        "L0_gnn_bx2": _L0_gnn_in["bx2"],
        "L0_gnn_Wn1": _L0_gnn_in["Wn1"],
        "L0_gnn_bn1": _L0_gnn_in["bn1"],
        "L0_gnn_Wn2": _L0_gnn_in["Wn2"],
        "L0_gnn_bn2": _L0_gnn_in["bn2"],
        "L0_gnn_We": _L0_gnn_in["We"],
        "L0_gnn_be": _L0_gnn_in["be"],
        "L0_gnn_Wv": _L0_gnn_in["Wv"],
        "L0_gnn_bv": _L0_gnn_in["bv"],
        "L0_gnn_Wfe": _L0_gnn_in["Wfe"],
        "L0_gnn_bfe": _L0_gnn_in["bfe"],
        "L0_gnn_Wfx": _L0_gnn_in["Wfx"],
        "L0_gnn_bfx": _L0_gnn_in["bfx"],
        "L0_ffn_gate_w": _L0_ffn_in["gate_w"],
        "L0_ffn_gate_b": _L0_ffn_in["gate_b"],
        "L0_ffn_w1": _L0_ffn_in["w1"],
        "L0_ffn_b1": _L0_ffn_in["b1"],
        "L0_ffn_w2": _L0_ffn_in["w2"],
        "L0_ffn_b2": _L0_ffn_in["b2"],
        "L0_ffn_gamma": _L0_ffn_in["gamma"],
        "L0_ffn_beta": _L0_ffn_in["beta"],
        "L1_gnn_W": _L1_gnn_in["W"],
        "L1_gnn_a_src": _L1_gnn_in["a_src"],
        "L1_gnn_a_dst": _L1_gnn_in["a_dst"],
        "L1_ffn_gate_w": _L1_ffn_in["gate_w"],
        "L1_ffn_gate_b": _L1_ffn_in["gate_b"],
        "L1_ffn_W1": _L1_ffn_in["W1"],
        "L1_ffn_b1": _L1_ffn_in["b1"],
        "L1_ffn_W2": _L1_ffn_in["W2"],
        "L1_ffn_b2": _L1_ffn_in["b2"],
        "L2_gnn_w1": _L2_gnn_in["w1"],
        "L2_gnn_w2": _L2_gnn_in["w2"],
        "L2_gnn_w3": _L2_gnn_in["w3"],
        "L2_gnn_bias": _L2_gnn_in["bias"],
        "L2_ffn_Wr": _L2_ffn_in["Wr"],
        "L2_ffn_W1s": _L2_ffn_in["W1s"],
        "L2_ffn_b1s": _L2_ffn_in["b1s"],
        "L2_ffn_W2s": _L2_ffn_in["W2s"],
        "L2_ffn_b2s": _L2_ffn_in["b2s"],
        "L2_ffn_W1p": _L2_ffn_in["W1p"],
        "L2_ffn_b1p": _L2_ffn_in["b1p"],
        "L2_ffn_W2p": _L2_ffn_in["W2p"],
        "L2_ffn_b2p": _L2_ffn_in["b2p"],
        "L3_gnn_W": _L3_gnn_in["W"],
        "L3_gnn_a": _L3_gnn_in["a"],
        "L3_gnn_wtrans": _L3_gnn_in["wtrans"],
        "L3_ffn_gate_w": _L3_ffn_in["gate_w"],
        "L3_ffn_gate_b": _L3_ffn_in["gate_b"],
        "L3_ffn_w1": _L3_ffn_in["w1"],
        "L3_ffn_w2": _L3_ffn_in["w2"],
        "L3_ffn_w3": _L3_ffn_in["w3"],
    }

def reference(x, adj, L0_gnn_neigh, L0_gnn_edge_emb, L0_gnn_Wx1, L0_gnn_bx1, L0_gnn_Wx2, L0_gnn_bx2, L0_gnn_Wn1, L0_gnn_bn1, L0_gnn_Wn2, L0_gnn_bn2, L0_gnn_We, L0_gnn_be, L0_gnn_Wv, L0_gnn_bv, L0_gnn_Wfe, L0_gnn_bfe, L0_gnn_Wfx, L0_gnn_bfx, L0_ffn_gate_w, L0_ffn_gate_b, L0_ffn_w1, L0_ffn_b1, L0_ffn_w2, L0_ffn_b2, L0_ffn_gamma, L0_ffn_beta, L1_gnn_W, L1_gnn_a_src, L1_gnn_a_dst, L1_ffn_gate_w, L1_ffn_gate_b, L1_ffn_W1, L1_ffn_b1, L1_ffn_W2, L1_ffn_b2, L2_gnn_w1, L2_gnn_w2, L2_gnn_w3, L2_gnn_bias, L2_ffn_Wr, L2_ffn_W1s, L2_ffn_b1s, L2_ffn_W2s, L2_ffn_b2s, L2_ffn_W1p, L2_ffn_b1p, L2_ffn_W2p, L2_ffn_b2p, L3_gnn_W, L3_gnn_a, L3_gnn_wtrans, L3_ffn_gate_w, L3_ffn_gate_b, L3_ffn_w1, L3_ffn_w2, L3_ffn_w3):
    import jax
    import jax.numpy as jnp
    def _L0_gnn_ref(x, neigh, edge_emb, adj, Wx1, bx1, Wx2, bx2, Wn1, bn1, Wn2, bn2, We, be, Wv, bv, Wfe, bfe, Wfx, bfx):
        import jax, jax.numpy as jnp
        import numpy as np
        N_NODES = 1024
        IN_DIM = 256
        EDGE_DIM = 32
        HID = 32
        OUT_DIM = 128
        N_EDGE_EMB = 100000
        neib_att = jnp.tanh(neigh @ Wn1 + bn1) @ Wn2 + bn2
        x_att = jnp.tanh(x @ Wx1 + bx1) @ Wx2 + bx2
        value = neigh @ Wv + bv
        edges = edge_emb[adj]
        e_att = jnp.tanh(edges @ We + be)
        ws = x_att @ neib_att.T + jnp.einsum('nkh,nh->nk', e_att, x_att)
        ws = jax.nn.leaky_relu(ws, 0.01)
        ws = jnp.where(adj > 0, ws, jnp.float32(-9000000000000000.0))
        ws = jax.nn.softmax(ws, axis=1)
        agg = ws @ value + jnp.einsum('nk,nko->no', ws, edges @ Wfe + bfe)
        return jnp.concatenate([x @ Wfx + bfx, agg], axis=1)

    def _L0_ffn_ref(x, gate_w, gate_b, w1, b1, w2, b2, gamma, beta):
        import jax, jax.numpy as jnp
        import numpy as np
        B, S, H, F, E, K = (8, 4096, 256, 512, 16, 2)
        EPS = 1e-05
        gate_logits = x @ gate_w + gate_b
        topk_vals, topk_idx = jax.lax.top_k(gate_logits, K)
        topk_w = jax.nn.softmax(topk_vals, axis=-1)
        h = jax.nn.relu(jnp.einsum('bsh,ehf->bsef', x, w1) + b1)
        expert_out = jnp.einsum('bsef,efh->bseh', h, w2) + b2
        sel = jnp.take_along_axis(expert_out, topk_idx[:, :, :, None], axis=2)
        moe = jnp.sum(topk_w[..., None] * sel, axis=2)
        y = x + moe
        mu = jnp.mean(y, axis=-1, keepdims=True)
        var = jnp.var(y, axis=-1, keepdims=True)
        return (y - mu) / jnp.sqrt(var + EPS) * gamma + beta

    def _L1_gnn_ref(x, adj, W, a_src, a_dst):
        import jax, jax.numpy as jnp
        import numpy as np
        N, IN_DIM, HEADS, OUT_DIM = (6144, 256, 4, 64)
        n = x.shape[0]
        heads, out_dim = a_src.shape
        h = (x @ W.T).reshape(n, heads, out_dim)
        e_src = jnp.einsum('nhd,hd->nh', h, a_src)
        e_dst = jnp.einsum('nhd,hd->nh', h, a_dst)
        e = jax.nn.leaky_relu(e_src[:, None, :] + e_dst[None, :, :], negative_slope=0.2)
        mask = (adj > 0)[:, :, None]
        e = jnp.where(mask, e, -jnp.inf)
        alpha = jax.nn.softmax(e, axis=1)
        out = jnp.einsum('ijh,jhd->ihd', alpha, h).reshape(n, heads * out_dim)
        return out

    def _L1_ffn_ref(x, gate_w, gate_b, W1, b1, W2, b2):
        import jax, jax.numpy as jnp
        import numpy as np
        B, T, D, H, E = (16, 4096, 256, 512, 8)
        Bb, Tt, Dd = x.shape
        Ee = gate_w.shape[1]
        xf = x.reshape(-1, Dd)
        N = xf.shape[0]
        logits = xf @ gate_w + gate_b
        probs = jax.nn.softmax(logits, axis=-1)
        top2_vals, top2_idx = jax.lax.top_k(probs, 2)
        cw = jnp.zeros((N, Ee), dtype=xf.dtype).at[jnp.arange(N)[:, None], top2_idx].add(top2_vals)

        def step(acc, params):
            w1, bb1, w2, bb2, we = params
            h = jax.nn.gelu(xf @ w1 + bb1, approximate=False)
            y = h @ w2 + bb2
            return (acc + we[:, None] * y, None)
        out, _ = jax.lax.scan(step, jnp.zeros_like(xf), (W1, b1, W2, b2, cw.T))
        return out.reshape(Bb, Tt, Dd)

    def _L2_gnn_ref(V, adj, w1, w2, w3, bias):
        import jax, jax.numpy as jnp
        import numpy as np
        N = 8192
        IN_F = 256
        OUT_F = 256
        o1 = jnp.matmul((adj == 1).astype(jnp.float32), jnp.matmul(V, w1))
        o2 = jnp.matmul((adj == 2).astype(jnp.float32), jnp.matmul(V, w2))
        o3 = jnp.matmul((adj == 3).astype(jnp.float32), jnp.matmul(V, w3))
        return o1 + o2 + o3 + bias

    def _L2_ffn_ref(x, Wr, W1s, b1s, W2s, b2s, W1p, b1p, W2p, b2p):
        import jax, jax.numpy as jnp
        import numpy as np
        B, S, D, F, E, K = (8, 2048, 256, 1024, 8, 2)
        gelu = lambda t: jax.nn.gelu(t, approximate=False)
        shared = gelu(x @ W1s + b1s) @ W2s + b2s
        rw = jax.nn.softmax(x @ Wr, axis=-1)
        topw, topi = jax.lax.top_k(rw, K)
        topw = topw / jnp.sum(topw, axis=-1, keepdims=True)
        mask = jnp.sum(jax.nn.one_hot(topi, E, dtype=topw.dtype) * topw[..., None], axis=-2)
        h = gelu(jnp.einsum('bsd,edf->bsef', x, W1p) + b1p)
        priv = jnp.einsum('bsef,efd->bsed', h, W2p) + b2p
        routed = jnp.einsum('bsed,bse->bsd', priv, mask)
        return shared + routed

    def _L3_gnn_ref(inp, adj, W, a, wtrans):
        import jax, jax.numpy as jnp
        import numpy as np
        N = 8192
        IN_F = 256
        OUT_F = 256
        ALPHA = 0.2
        NEG_INF = -1000000000000.0
        h = inp @ W
        Wh1 = h @ a[:OUT_F, :]
        Wh2 = h @ a[OUT_F:, :]
        e = jax.nn.leaky_relu(Wh1 + Wh2.T, ALPHA)
        mask = adj > 0
        attention = jax.nn.softmax(jnp.where(mask, e, NEG_INF), axis=1)
        negative_attention = -jax.nn.softmax(jnp.where(mask, -e, NEG_INF), axis=1)
        h_prime = attention @ inp
        h_prime_negative = negative_attention @ inp
        h_prime_double = jnp.concatenate([h_prime, h_prime_negative], axis=1)
        new_h_prime = h_prime_double @ wtrans
        return jax.nn.elu(new_h_prime)

    def _L3_ffn_ref(x, gate_w, gate_b, w1, w2, w3):
        import jax, jax.numpy as jnp
        import numpy as np
        D_MODEL = 256
        N_EXPERTS = 16
        HIDDEN = 512
        SCALE = 0.02
        n_experts = w1.shape[0]
        logits = jnp.einsum('bsd,de->bse', x, gate_w) + gate_b
        probs = jax.nn.softmax(logits, axis=-1)
        top_probs, top_idx = jax.lax.top_k(probs, 2)
        top_probs = top_probs / jnp.sum(top_probs, axis=-1, keepdims=True)
        dispatch = jnp.sum(jax.nn.one_hot(top_idx, n_experts, dtype=x.dtype) * top_probs[..., None], axis=-2)
        h1 = jnp.einsum('bsd,edh->bseh', x, w1)
        h2 = jnp.einsum('bsd,edh->bseh', x, w2)
        hidden = jax.nn.silu(h1) * h2
        expert_out = jnp.einsum('bseh,eho->bseo', hidden, w3)
        return jnp.einsum('bseo,bse->bso', expert_out, dispatch)

    x = x + _L0_gnn_ref(_layernorm(x, axis=-1), L0_gnn_neigh, L0_gnn_edge_emb, adj, L0_gnn_Wx1, L0_gnn_bx1, L0_gnn_Wx2, L0_gnn_bx2, L0_gnn_Wn1, L0_gnn_bn1, L0_gnn_Wn2, L0_gnn_bn2, L0_gnn_We, L0_gnn_be, L0_gnn_Wv, L0_gnn_bv, L0_gnn_Wfe, L0_gnn_bfe, L0_gnn_Wfx, L0_gnn_bfx)
    x = x + _L0_ffn_ref((_layernorm(x, axis=-1))[None], L0_ffn_gate_w, L0_ffn_gate_b, L0_ffn_w1, L0_ffn_b1, L0_ffn_w2, L0_ffn_b2, L0_ffn_gamma, L0_ffn_beta)[0]
    x = x + _L1_gnn_ref(_layernorm(x, axis=-1), adj, L1_gnn_W, L1_gnn_a_src, L1_gnn_a_dst)
    x = x + _L1_ffn_ref((_layernorm(x, axis=-1))[None], L1_ffn_gate_w, L1_ffn_gate_b, L1_ffn_W1, L1_ffn_b1, L1_ffn_W2, L1_ffn_b2)[0]
    x = x + _L2_gnn_ref(_layernorm(x, axis=-1), adj, L2_gnn_w1, L2_gnn_w2, L2_gnn_w3, L2_gnn_bias)
    x = x + _L2_ffn_ref((_layernorm(x, axis=-1))[None], L2_ffn_Wr, L2_ffn_W1s, L2_ffn_b1s, L2_ffn_W2s, L2_ffn_b2s, L2_ffn_W1p, L2_ffn_b1p, L2_ffn_W2p, L2_ffn_b2p)[0]
    x = x + _L3_gnn_ref(_layernorm(x, axis=-1), adj, L3_gnn_W, L3_gnn_a, L3_gnn_wtrans)
    x = x + _L3_ffn_ref((_layernorm(x, axis=-1))[None], L3_ffn_gate_w, L3_ffn_gate_b, L3_ffn_w1, L3_ffn_w2, L3_ffn_w3)[0]
    return x


_drawn_inputs = setup_inputs


def setup_inputs(seed=0):
    import zlib

    import numpy as np

    out = dict(_drawn_inputs(seed))
    spreads = {'L0_gnn_bx1': (0.0, 0.8),
     'L0_gnn_bx2': (0.0, 0.8),
     'L0_gnn_bn1': (0.0, 0.8),
     'L0_gnn_bn2': (0.0, 2.0),
     'L0_gnn_be': (0.0, 2.0),
     'L0_gnn_bv': (0.0, 0.1),
     'L0_gnn_bfe': (0.0, 0.1),
     'L0_gnn_bfx': (0.0, 0.1),
     'L0_ffn_gate_b': (0.0, 0.1),
     'L0_ffn_b1': (0.0, 0.543),
     'L0_ffn_b2': (0.0, 0.1),
     'L0_ffn_gamma': (1.0, 0.2),
     'L0_ffn_beta': (0.0, 0.1),
     'L1_ffn_gate_b': (0.0, 0.8),
     'L1_ffn_b1': (0.0, 0.8),
     'L1_ffn_b2': (0.0, 0.344),
     'L2_ffn_b1s': (0.0, 0.8),
     'L2_ffn_b2s': (0.0, 0.8),
     'L2_ffn_b1p': (0.0, 0.8),
     'L2_ffn_b2p': (0.0, 0.8),
     'L3_ffn_gate_b': (0.0, 0.8)}
    factors = {'L0_gnn_Wx1': 8.0,
     'L0_gnn_Wx2': 8.0,
     'L0_gnn_Wn1': 8.0,
     'L0_gnn_Wn2': 8.0,
     'L0_gnn_We': 27.524,
     'L0_ffn_w1': 3.106,
     'L1_gnn_a_src': 6.251,
     'L1_ffn_gate_w': 5.717,
     'L1_ffn_W1': 8.0,
     'L1_ffn_W2': 5.892,
     'L2_gnn_bias': 8.0,
     'L2_ffn_Wr': 5.162,
     'L2_ffn_W1s': 5.239,
     'L2_ffn_W2s': 4.755,
     'L2_ffn_W1p': 7.059,
     'L2_ffn_W2p': 6.47,
     'L3_gnn_W': 6.108,
     'L3_gnn_a': 6.669,
     'L3_ffn_gate_w': 8.0,
     'L3_ffn_w1': 8.0,
     'L3_ffn_w2': 8.0,
     'L3_ffn_w3': 8.0}
    for name, (base, spread) in spreads.items():
        noise = np.random.default_rng([zlib.crc32(name.encode()), seed]).standard_normal(out[name].shape)
        drawn = base * np.exp(spread * noise) if base else spread * noise
        out[name] = jnp.asarray(drawn.astype(out[name].dtype))
    for name, factor in factors.items():
        out[name] = (out[name] * factor).astype(out[name].dtype)
    return out
```

```python
import concourse.bass as bass
from concourse import mybir
from contextlib import ExitStack

P = 128
N = 1024
NT = N // P
D = 256
DC = D // P
EPS = 1e-5
MASKED = -1e30
UN = 4


def build(nc, A, out, stop=99):
    F32, BF16, I32, U32 = mybir.dt.float32, mybir.dt.bfloat16, mybir.dt.int32, mybir.dt.uint32
    ALU, ACT, AX = mybir.AluOpType, mybir.ActivationFunctionType, mybir.AxisListType

    def max_tiles(experts):
        return (2 * N + experts * (P - 1)) // P

    SLOTS = max(max_tiles(16), max_tiles(8) + NT) * P
    x_slots = nc.dram_tensor("x_slots", [SLOTS, D], F32, kind="Internal").ap()
    y_slots = nc.dram_tensor("y_slots", [SLOTS, D], F32, kind="Internal").ap()

    top = ExitStack()
    with top:
        def keep(name, shape, dt=F32):
            return top.enter_context(nc.sbuf_tensor(name, shape, dt))

        x = keep("x", [P, NT, D])
        xn = keep("xn", [P, NT, D + 1])
        xnT = keep("xnT", [P, DC, N])
        neg = keep("neg", [P, NT, N])
        ident = keep("ident", [P, P])
        ones_f = keep("ones_f", [P, P])
        ones_b = keep("ones_b", [P, P], BF16)
        before_b = keep("before_b", [P, P], BF16)
        iota_f = keep("iota_f", [P, 32])
        iota_128 = keep("iota_128", [P, NT])
        before_e = keep("before_e", [P, 16, 16])
        stats = keep("stats", [P, NT, 6])
        mean_var = keep("mean_var", [P, NT, 2])
        rstd = keep("rstd", [P, NT, 1])
        power = keep("power", [P, NT, 1])
        pos = keep("pos", [P, 2, NT], U32)
        wts = keep("wts", [P, 2, NT])
        etab = keep("etab", [1, 32], I32)

        sems = []

        class Phase:

            def __init__(self, name):
                self.name, self.ctx = name, ExitStack()

            def __enter__(self):
                return self

            def sb(self, name, shape, dt=F32):
                return self.ctx.enter_context(nc.sbuf_tensor(f"{self.name}_{name}", shape, dt))

            def ps(self, name, shape, dt=F32):
                return self.ctx.enter_context(nc.psum_tensor(f"{self.name}_{name}", shape, dt))

            def sem(self, name):
                sems.append(nc.alloc_semaphore(f"{self.name}_{name}"))
                return sems[-1]

            def block(self):
                return self.ctx.enter_context(nc.Block(no_gpsimd_drain=True))

            def __exit__(self, *a):
                return self.ctx.__exit__(*a)

        def linker(eng, sem):
            count = [0]

            def link(ins):
                count[0] += 1
                ins.then_inc(sem, 1)
                eng.wait_ge(sem, count[0])
            return link

        def bc(ap, shape):
            return ap.to_broadcast(shape)

        def norm_gpsimd(pool, var_ready, rstd_ready):
            pool.wait_ge(var_ready, 1)
            nc.gpsimd.tensor_scalar(mean_var[:, :, 1:2], mean_var[:, :, 1:2], EPS, None, ALU.add)\
                .then_inc(rstd_ready, 1)
            pool.wait_ge(rstd_ready, 1)
            nc.gpsimd.tensor_tensor(rstd[:, :, :], mean_var[:, :, 1:2], power[:, :, :], ALU.pow)\
                .then_inc(rstd_ready, 1)

        def norm_vector(dve, link, var_ready, rstd_ready, xn_ready):
            for t in range(NT):
                ins = nc.vector.bn_stats(out=stats[:, t, :], in_=x[:, t, :])
            link(ins)
            for t in range(NT):
                ins = nc.vector.bn_aggr(out=mean_var[:, t, :], in_=stats[:, t, :])
            ins.then_inc(var_ready, 1)
            dve.wait_ge(rstd_ready, 2)
            for t in range(NT):
                nc.vector.tensor_scalar(xn[:, t, 0:D], x[:, t, :], mean_var[:, t, 0:1], rstd[:, t, :],
                                        ALU.subtract, ALU.mult).then_inc(xn_ready, 1)

        def norm_tensor(pe, tps, xn_ready, tp_ready, xnT_ready):
            for t in range(NT):
                pe.wait_ge(xn_ready, t + 1)
                if t >= 2:
                    pe.wait_ge(xnT_ready, t - 1)
                for c in range(DC):
                    ins = nc.tensor.transpose(tps[t % 2][:, c, :], xn[:, t, c * P:(c + 1) * P], ident[:, :])
                ins.then_inc(tp_ready, 1)

        def norm_scalar(act, tps, tp_ready, xnT_ready):
            for t in range(NT):
                act.wait_ge(tp_ready, t + 1)
                nc.scalar.activation(xnT[:, :, t * P:(t + 1) * P], tps[t % 2][:, :, :], ACT.Copy)\
                    .then_inc(xnT_ready, 1)

        with Phase("init") as ph:
            adj = ph.sb("adj", [P, NT, N], I32)
            iota_i = ph.sb("iota_i", [P, 32], I32)
            zero = ph.sb("zero", [P, SLOTS // P * 64])
            loaded, adj_loaded, zeroed = ph.sem("loaded"), ph.sem("adj_loaded"), ph.sem("zeroed")
            made, made_v, zero_made = ph.sem("made"), ph.sem("made_v"), ph.sem("zero_made")
            block = ph.block()

            @block.sync
            def _(sp):
                sp.dma_start(x[:, :, :], A["x"].rearrange("(t p) d -> p t d", p=P)).then_inc(loaded, 16)
                sp.dma_start(adj[:, :, :], A["adj"].rearrange("(t p) k -> p t k", p=P)).then_inc(adj_loaded, 16)
                sp.wait_ge(zero_made, 1)
                for q in range(4):
                    sp.dma_start(x_slots.rearrange("(p r) (q d) -> q p r d", p=P, q=4)[q],
                                 zero[:, :].rearrange("p (r d) -> p r d", d=64)).then_inc(zeroed, 16)
                sp.wait_ge(loaded, 16)
                sp.wait_ge(zeroed, 64)

            @block.gpsimd
            def _(pool):
                link = linker(pool, made)
                link(nc.gpsimd.memset(ident[:, :], 0.0))
                nc.gpsimd.affine_select(out=ident[:, :], in_=ident[:, :], compare_op=ALU.not_equal, fill=1.0,
                                        base=0, pattern=[[-1, P]], channel_multiplier=1)
                link(nc.gpsimd.memset(before_b[:, :], 1.0))
                nc.gpsimd.affine_select(out=before_b[:, :], in_=before_b[:, :], compare_op=ALU.is_gt, fill=0.0,
                                        base=0, pattern=[[1, P]], channel_multiplier=-1)
                link(nc.gpsimd.iota(iota_i[:, :], pattern=[[1, 32]], base=0, channel_multiplier=0))

            @block.vector
            def _(dve):
                link = linker(dve, made_v)
                nc.vector.memset(zero[:, :], 0.0).then_inc(zero_made, 1)
                nc.vector.memset(ones_f[:, :], 1.0)
                nc.vector.memset(power[:, :, :], -0.5)
                nc.vector.memset(ones_b[:, :], 1.0)
                nc.vector.memset(xn[:, :, D:D + 1], 1.0)
                dve.wait_ge(made, 3)
                link(nc.vector.tensor_copy(iota_f[:, :], iota_i[:, :]))
                nc.vector.tensor_scalar(iota_128[:, :], iota_f[:, 0:NT], float(P), None, ALU.mult)
                nc.vector.tensor_tensor(before_e[:, :, :], bc(iota_f[:, 0:16].unsqueeze(1), [P, 16, 16]),
                                        bc(iota_f[:, 0:16].unsqueeze(2), [P, 16, 16]), ALU.is_lt)
                dve.wait_ge(adj_loaded, 16)
                nc.vector.tensor_scalar(neg[:, :, :], adj[:, :, :], 0.0, MASKED, ALU.is_le, ALU.mult)

        def attention(block, ph, heads, slope, lowest, rows, s, sa, values, width, finish,
                      scores=None, extra=()):
            units = NT * heads
            g = [ph.sb(f"g{n}", [P, N]) for n in range(3)]
            t2 = [ph.sb(f"t2{n}", [P, N]) for n in range(3)]
            lm = [ph.sb(f"lm{n}", [P, N]) for n in range(2)]
            pT = [ph.sb(f"pT{n}", [P, NT, P]) for n in range(2)]
            small = ph.sb("small", [P, 6, units])
            gm, y, ay, m, b1, b2 = (small[:, n, :] for n in range(6))
            tp = [ph.ps(f"tp{n}", [P, NT, P]) for n in range(2)]
            o = [ph.ps(f"o{n}", [P, 512]) for n in range(2)]
            scored, maxed, biased = ph.sem("scored"), ph.sem("maxed"), ph.sem("biased")
            sloped, shifted, turned = ph.sem("sloped"), ph.sem("shifted"), ph.sem("turned")
            exped, weighed, finished = ph.sem("exped"), ph.sem("weighed"), ph.sem("finished")
            pool_done, vec_done = ph.sem("pool_done"), ph.sem("vec_done")

            @block.vector
            def _(dve):
                link = linker(dve, vec_done)
                if "vector" in extra:
                    extra["vector"](dve, link)

                def mask(u):
                    if u >= 3:
                        dve.wait_ge(sloped, u - 2)
                        dve.wait_ge(shifted, u - 2)
                    if scores:
                        dve.wait_ge(scored, u + 1)
                    nc.vector.tensor_tensor_reduce(
                        out=g[u % 3][:, :], in0=rows(u), in1=neg[:, u // heads, :], scale=1.0, scalar=-3e38,
                        op0=ALU.add, op1=ALU.max, accum_out=gm[:, u:u + 1]).then_inc(maxed, 1)

                def shift(u):
                    dve.wait_ge(sloped, u + 1)
                    if u >= 2:
                        dve.wait_ge(turned, 2 * (u - 1))
                    nc.vector.scalar_tensor_tensor(
                        out=lm[u % 2][:, :], in0=g[u % 3][:, :], scalar=b1[:, u:u + 1], in1=t2[u % 3][:, :],
                        op0=ALU.add, op1=ALU.min if lowest(u) else ALU.max).then_inc(shifted, 1)

                def end(u):
                    dve.wait_ge(weighed, u + 1)
                    finish(u, dve, link, o[u % 2]).then_inc(finished, 1)

                for u in range(units + 3):
                    if u < units:
                        mask(u)
                    if 1 <= u <= units:
                        shift(u - 1)
                    if u >= 3:
                        end(u - 3)
                if "vector_end" in extra:
                    link(nc.vector.memset(stats[:, 0, 0:1], 0.0))
                    extra["vector_end"](dve, link, gm)

            @block.gpsimd
            def _(pool):
                link = linker(pool, pool_done)
                if "pool" in extra:
                    extra["pool"](pool)
                for u in range(units):
                    c = slice(u, u + 1)
                    pool.wait_ge(maxed, u + 1)
                    link(nc.gpsimd.tensor_tensor(y[:, c], gm[:, c], s[:, c], ALU.add))
                    nc.gpsimd.tensor_scalar(ay[:, c], y[:, c], slope, None, ALU.mult)
                    link(nc.gpsimd.tensor_scalar(m[:, c], y[:, c], 0.0, 1.0 - slope,
                                                 ALU.min if lowest(u) else ALU.max, ALU.mult))
                    link(nc.gpsimd.tensor_tensor(m[:, c], m[:, c], ay[:, c], ALU.add))
                    nc.gpsimd.tensor_tensor(b1[:, c], s[:, c], m[:, c], ALU.subtract)
                    nc.gpsimd.tensor_tensor(b2[:, c], sa[:, c], m[:, c], ALU.subtract).then_inc(biased, 1)

            @block.scalar
            def _(act):
                if "scalar" in extra:
                    extra["scalar"](act)

                def slope_of(u):
                    act.wait_ge(biased, u + 1)
                    if u >= 3:
                        act.wait_ge(shifted, u - 2)
                    nc.scalar.activation(t2[u % 3][:, :], g[u % 3][:, :], ACT.Identity, bias=b2[:, u:u + 1],
                                         scale=slope).then_inc(sloped, 1)

                def exp_of(u):
                    for hf in range(2):
                        act.wait_ge(turned, 2 * u + hf + 1)
                        if u >= 2 and hf == 0:
                            act.wait_ge(weighed, u - 1)
                        q = slice(hf * NT // 2, (hf + 1) * NT // 2)
                        nc.scalar.activation(pT[u % 2][:, q, :], tp[u % 2][:, q, :], ACT.Exp)\
                            .then_inc(exped, 1)

                for u in range(units + 2):
                    if u < units:
                        slope_of(u)
                    if u >= 2:
                        exp_of(u - 2)

            @block.tensor
            def _(pe):
                if "tensor" in extra:
                    extra["tensor"](pe)

                def turn(u):
                    pe.wait_ge(shifted, u + 1)
                    for hf in range(2):
                        if u >= 2:
                            pe.wait_ge(exped, 2 * (u - 2) + hf + 1)
                        for c in range(hf * NT // 2, (hf + 1) * NT // 2):
                            ins = nc.tensor.transpose(tp[u % 2][:, c, :], lm[u % 2][:, c * P:(c + 1) * P],
                                                      ident[:, :])
                        ins.then_inc(turned, 1)

                def weigh(u):
                    if u >= 2:
                        pe.wait_ge(finished, u - 1)
                    for c in range(NT):
                        if c % (NT // 2) == 0:
                            pe.wait_ge(exped, 2 * u + c // (NT // 2) + 1)
                        ins = nc.tensor.matmul(o[u % 2][:, 0:width], pT[u % 2][:, c, :], values(u, c),
                                               start=(c == 0), stop=(c == NT - 1))
                    ins.then_inc(weighed, 1)

                for u in range(units + 2):
                    if scores and u < units:
                        if u >= 1:
                            pe.wait_ge(maxed, u)
                        scores(u).then_inc(scored, 1)
                    if 1 <= u <= units:
                        turn(u - 1)
                    if u >= 2:
                        weigh(u - 2)
                if "tensor_end" in extra:
                    extra["tensor_end"](pe)

        def graph0():
            HID, OUT, ED = 32, 128, 32
            with Phase("g0") as ph:
                s = ph.sb("s", [P, NT])
                sa = ph.sb("sa", [P, NT])
                xa = ph.sb("xa", [HID, N])
                na = ph.sb("na", [HID, N])
                V = ph.sb("V", [P, NT, OUT + 1])
                f01 = ph.sb("f01", [P, 2, OUT])
                with Phase("p0") as pp:
                    neighT = pp.sb("neighT", [P, DC, N])
                    wx1, wn1 = pp.sb("wx1", [P, DC, HID]), pp.sb("wn1", [P, DC, HID])
                    wx2, wn2, we = (pp.sb(n, [HID, HID]) for n in ("wx2", "wn2", "we"))
                    cols = pp.sb("cols", [HID, 5])
                    wv, wfx = pp.sb("wv", [P, DC, OUT]), pp.sb("wfx", [P, DC, OUT])
                    wfe = pp.sb("wfe", [ED, OUT])
                    emb = pp.sb("emb", [ED, 2])
                    rowsb = pp.sb("rowsb", [P, 3, OUT])
                    emb_b = pp.sb("emb_b", [ED, 2, P])
                    tx, tn = pp.sb("tx", [HID, N]), pp.sb("tn", [HID, N])
                    eatt = pp.sb("eatt", [HID, 2])
                    tps = [pp.ps(f"tps{n}", [P, DC, P]) for n in range(2)]
                    psA = pp.ps("psA", [P, 2, 512])
                    psB = pp.ps("psB", [P, 2, 512])
                    loaded = pp.sem("loaded")
                    var_ready, rstd_ready = pp.sem("var_ready"), pp.sem("rstd_ready")
                    xn_ready, tp_ready, xnT_ready = pp.sem("xn"), pp.sem("tp"), pp.sem("xnT")
                    vd, mm, copied, tanhed = pp.sem("vd"), pp.sem("mm"), pp.sem("copied"), pp.sem("tanhed")
                    blk = pp.block()
                    loads = [(neighT[:, :, :], A["neighT"].rearrange("(c p) n -> p c n", p=P))]
                    loads += [(w[:, :, :], A[n].rearrange("(c p) n -> p c n", p=P)) for w, n in
                              ((wx1, "L0_gnn_Wx1"), (wn1, "L0_gnn_Wn1"), (wv, "L0_gnn_Wv"), (wfx, "L0_gnn_Wfx"))]
                    loads += [(w[:, :], A[n]) for w, n in ((wx2, "L0_gnn_Wx2"), (wn2, "L0_gnn_Wn2"),
                                                           (we, "L0_gnn_We"), (wfe, "L0_gnn_Wfe"))]
                    loads += [(cols[:, n:n + 1], A[b].unsqueeze(1)) for n, b in
                              enumerate(("L0_gnn_bx1", "L0_gnn_bx2", "L0_gnn_bn1", "L0_gnn_bn2", "L0_gnn_be"))]
                    loads += [(rowsb[:, n, :], A[b].unsqueeze(0).to_broadcast([P, OUT])) for n, b in
                              enumerate(("L0_gnn_bv", "L0_gnn_bfx", "L0_gnn_bfe"))]
                    loads += [(emb[:, n:n + 1], A["L0_gnn_edge_emb"][n, :].unsqueeze(1)) for n in range(2)]
                    ALL = 16 * len(loads)

                    @blk.sync
                    def _(sp):
                        for dst, src in loads:
                            sp.dma_start(dst, src).then_inc(loaded, 16)
                        sp.wait_ge(loaded, ALL)

                    @blk.tensor
                    def _(pe):
                        norm_tensor(pe, tps, xn_ready, tp_ready, xnT_ready)
                        pe.wait_ge(loaded, ALL)
                        pe.wait_ge(xnT_ready, NT)
                        for w, src, ps in ((wx1, xnT, psA), (wn1, neighT, psB)):
                            for hf in range(2):
                                for c in range(DC):
                                    ins = nc.tensor.matmul(ps[0:HID, hf, :], w[:, c, :],
                                                           src[:, c, hf * 512:(hf + 1) * 512],
                                                           start=(c == 0), stop=(c == DC - 1))
                            ins.then_inc(mm, 1)
                        for n, (w, src, ps) in enumerate(((wx2, tx, psA), (wn2, tn, psB))):
                            pe.wait_ge(tanhed, n + 1)
                            for hf in range(2):
                                ins = nc.tensor.matmul(ps[0:HID, hf, :], w[:, :], src[:, hf * 512:(hf + 1) * 512],
                                                       start=True, stop=True)
                            ins.then_inc(mm, 1)
                        pe.wait_ge(copied, 2)
                        nc.tensor.matmul(psA[0:HID, 0, 0:2], we[:, :], emb[:, :], start=True, stop=True)\
                            .then_inc(mm, 1)
                        pe.wait_ge(tanhed, 3)
                        for t in range(NT):
                            ins = nc.tensor.matmul(psA[:, 1, t:t + 1], xa[:, t * P:(t + 1) * P], eatt[:, 1:2],
                                                   start=True, stop=True)
                        ins.then_inc(mm, 1)
                        for n in range(2):
                            ins = nc.tensor.matmul(psB[:, 0, n * OUT:(n + 1) * OUT], emb_b[:, n, :], wfe[:, :],
                                                   start=True, stop=True)
                        ins.then_inc(mm, 1)
                        pe.wait_ge(copied, 4)
                        for t in range(NT):
                            if t >= 2:
                                pe.wait_ge(copied, 4 + t - 1)
                            ps = (psA, psB)[t % 2]
                            for n, (src, w) in enumerate(((neighT, wv), (xnT, wfx))):
                                for c in range(DC):
                                    ins = nc.tensor.matmul(ps[:, n, 0:OUT], src[:, c, t * P:(t + 1) * P], w[:, c, :],
                                                           start=(c == 0), stop=(c == DC - 1))
                            ins.then_inc(mm, 1)

                    @blk.gpsimd
                    def _(pool):
                        norm_gpsimd(pool, var_ready, rstd_ready)

                    @blk.scalar
                    def _(act):
                        norm_scalar(act, tps, tp_ready, xnT_ready)
                        act.wait_ge(loaded, ALL)
                        for n, (t, ps) in enumerate(((tx, psA), (tn, psB))):
                            act.wait_ge(mm, n + 1)
                            nc.scalar.activation(t[:, :].rearrange("p (a b) -> p a b", a=2), ps[0:HID, :, :],
                                                 ACT.Tanh, bias=cols[:, 2 * n:2 * n + 1]).then_inc(tanhed, 1)
                        act.wait_ge(mm, 5)
                        nc.scalar.activation(eatt[:, :], psA[0:HID, 0, 0:2], ACT.Tanh, bias=cols[:, 4:5])\
                            .then_inc(tanhed, 1)

                    @blk.vector
                    def _(dve):
                        link = linker(dve, vd)
                        norm_vector(dve, link, var_ready, rstd_ready, xn_ready)
                        nc.vector.memset(V[:, :, OUT:OUT + 1], 1.0)
                        dve.wait_ge(loaded, ALL)
                        nc.vector.tensor_copy(emb_b[:, 0, :], bc(emb[:, 0:1], [ED, P]))
                        link(nc.vector.tensor_copy(emb_b[:, 1, :], bc(emb[:, 1:2], [ED, P])))
                        for n, (t, ps) in enumerate(((xa, psA), (na, psB))):
                            dve.wait_ge(mm, 3 + n)
                            nc.vector.tensor_scalar(t[:, :].rearrange("p (a b) -> p a b", a=2), ps[0:HID, :, :],
                                                    cols[:, 2 * n + 1:2 * n + 2], None, ALU.add).then_inc(copied, 1)
                        dve.wait_ge(mm, 6)
                        nc.vector.tensor_copy(s[:, :], psA[:, 1, 0:NT])
                        nc.vector.tensor_scalar(sa[:, :], psA[:, 1, 0:NT], 0.01, None, ALU.mult).then_inc(copied, 1)
                        dve.wait_ge(mm, 7)
                        nc.vector.tensor_tensor(f01[:, :, :], psB[:, 0, 0:2 * OUT].rearrange("p (a b) -> p a b", a=2),
                                                bc(rowsb[:, 2:3, :], [P, 2, OUT]), ALU.add).then_inc(copied, 1)
                        for t in range(NT):
                            dve.wait_ge(mm, 8 + t)
                            ps = (psA, psB)[t % 2]
                            nc.vector.tensor_tensor(V[:, t, 0:OUT], ps[:, 0, 0:OUT], rowsb[:, 0, :], ALU.add)
                            link(nc.vector.tensor_tensor(x[:, t, 0:OUT], ps[:, 1, 0:OUT], x[:, t, 0:OUT], ALU.add))
                            nc.vector.tensor_tensor(x[:, t, 0:OUT], x[:, t, 0:OUT], rowsb[:, 1, :], ALU.add)\
                                .then_inc(copied, 1)

                S = ph.ps("S", [P, 2, 512])
                r = ph.sb("r", [P, NT])
                has = ph.sb("has", [P, NT])
                block = ph.block()

                def scores(u):
                    for hf in range(2):
                        ins = nc.tensor.matmul(S[:, hf, :], xa[:, u * P:(u + 1) * P],
                                               na[:, hf * 512:(hf + 1) * 512], start=True, stop=True)
                    return ins

                def finish(u, dve, link, o):
                    link(nc.vector.reciprocal(r[:, u:u + 1], o[:, OUT:OUT + 1]))
                    return nc.vector.scalar_tensor_tensor(
                        out=x[:, u, OUT:D], in0=o[:, 0:OUT], scalar=r[:, u:u + 1], in1=x[:, u, OUT:D],
                        op0=ALU.mult, op1=ALU.add)

                def vector_end(dve, link, gm):
                    nc.vector.tensor_scalar(has[:, :], gm, MASKED / 2, None, ALU.is_gt)
                    link(nc.vector.tensor_tensor(f01[:, 1, :], f01[:, 1, :], f01[:, 0, :], ALU.subtract))
                    link(nc.vector.tensor_tensor(x[:, :, OUT:D], x[:, :, OUT:D],
                                                 bc(f01[:, 0:1, :], [P, NT, OUT]), ALU.add))
                    for t in range(NT):
                        nc.vector.scalar_tensor_tensor(
                            out=x[:, t, OUT:D], in0=f01[:, 1, :], scalar=has[:, t:t + 1], in1=x[:, t, OUT:D],
                            op0=ALU.mult, op1=ALU.add)

                attention(block, ph, 1, 0.01, lambda u: False, lambda u: S[:, :, :].rearrange("p a b -> p (a b)"),
                          s, sa, lambda u, c: V[:, c, :], OUT + 1, finish, scores, {"vector_end": vector_end})

        def graph1():
            H, DH, SLOPE = 4, 64, 0.2
            with Phase("g1") as ph:
                s = ph.sb("s", [P, NT, H])
                sa = ph.sb("sa", [P, NT, H])
                dst = ph.sb("dst", [P, H, N])
                V = ph.sb("V", [P, NT, H, DH + 1])
                with Phase("p1") as pp:
                    hT = pp.sb("hT", [P, DC, N])
                    w = pp.sb("w", [P, DC, D])
                    a_src = pp.sb("a_src", [P, DC, H])
                    a_dst = pp.sb("a_dst", [P, H, 1])
                    a_dstb = pp.sb("a_dstb", [P, H, P])
                    tps = [pp.ps(f"tps{n}", [P, DC, P]) for n in range(2)]
                    ps = [pp.ps(f"ps{n}", [P, 512]) for n in range(4)]
                    loaded, zeroed = pp.sem("loaded"), pp.sem("zeroed")
                    var_ready, rstd_ready = pp.sem("var_ready"), pp.sem("rstd_ready")
                    xn_ready, tp_ready, xnT_ready = pp.sem("xn"), pp.sem("tp"), pp.sem("xnT")
                    vd, mm, copied, spread = pp.sem("vd"), pp.sem("mm"), pp.sem("copied"), pp.sem("spread")
                    blk = pp.block()
                    ALL = 16 * (1 + 2 * H)

                    @blk.sync
                    def _(sp):
                        sp.dma_start(w[:, :, :], A["L1_gnn_WT"].rearrange("(c p) n -> p c n", p=P)).then_inc(loaded, 16)
                        sp.wait_ge(zeroed, 1)
                        for h in range(H):
                            part = slice(h % 2 * DH, (h % 2 + 1) * DH)
                            sp.dma_start(a_src[part, h // 2, h:h + 1], A["L1_gnn_a_src"][h, :].unsqueeze(1))\
                                .then_inc(loaded, 16)
                            sp.dma_start(a_dst[part, h, :], A["L1_gnn_a_dst"][h, :].unsqueeze(1)).then_inc(loaded, 16)
                        sp.wait_ge(loaded, ALL)

                    @blk.tensor
                    def _(pe):
                        norm_tensor(pe, tps, xn_ready, tp_ready, xnT_ready)
                        pe.wait_ge(loaded, ALL)
                        pe.wait_ge(xnT_ready, NT)
                        n = 0
                        for fc in range(DC):
                            for hf in range(2):
                                for c in range(DC):
                                    ins = nc.tensor.matmul(ps[n % 4][:, :], w[:, c, fc * P:(fc + 1) * P],
                                                           xnT[:, c, hf * 512:(hf + 1) * 512],
                                                           start=(c == 0), stop=(c == DC - 1))
                                ins.then_inc(mm, 1)
                                n += 1
                        for t in range(NT):
                            pe.wait_ge(copied, n - 3)
                            for c in range(DC):
                                ins = nc.tensor.matmul(ps[n % 4][:, 0:D], xnT[:, c, t * P:(t + 1) * P], w[:, c, :],
                                                       start=(c == 0), stop=(c == DC - 1))
                            ins.then_inc(mm, 1)
                            n += 1
                        pe.wait_ge(spread, 1)
                        for h in range(H):
                            for hf in range(2):
                                pe.wait_ge(copied, n - 3)
                                nc.tensor.matmul(ps[n % 4][:, :], a_dstb[:, h, :], hT[:, h // 2, hf * 512:(hf + 1) * 512],
                                                 start=True, stop=True).then_inc(mm, 1)
                                n += 1
                        pe.wait_ge(copied, n - 3)
                        for t in range(NT):
                            for fc in range(DC):
                                ins = nc.tensor.matmul(ps[n % 4][:, t * H:(t + 1) * H], hT[:, fc, t * P:(t + 1) * P],
                                                       a_src[:, fc, :], start=(fc == 0), stop=(fc == DC - 1))
                        ins.then_inc(mm, 1)

                    @blk.gpsimd
                    def _(pool):
                        norm_gpsimd(pool, var_ready, rstd_ready)

                    @blk.scalar
                    def _(act):
                        norm_scalar(act, tps, tp_ready, xnT_ready)

                    @blk.vector
                    def _(dve):
                        link = linker(dve, vd)
                        nc.vector.memset(a_src[:, :, :], 0.0)
                        nc.vector.memset(a_dst[:, :, :], 0.0).then_inc(zeroed, 1)
                        norm_vector(dve, link, var_ready, rstd_ready, xn_ready)
                        nc.vector.memset(V[:, :, :, DH:DH + 1], 1.0)
                        dve.wait_ge(loaded, ALL)
                        nc.vector.tensor_copy(a_dstb[:, :, :], bc(a_dst[:, :, :], [P, H, P])).then_inc(spread, 1)
                        n = 0
                        for fc in range(DC):
                            for hf in range(2):
                                dve.wait_ge(mm, n + 1)
                                nc.vector.tensor_copy(hT[:, fc, hf * 512:(hf + 1) * 512], ps[n % 4][:, :])\
                                    .then_inc(copied, 1)
                                n += 1
                        for t in range(NT):
                            dve.wait_ge(mm, n + 1)
                            nc.vector.tensor_copy(V[:, t, :, 0:DH],
                                                  ps[n % 4][:, 0:D].rearrange("p (h d) -> p h d", h=H)).then_inc(copied, 1)
                            n += 1
                        for h in range(H):
                            for hf in range(2):
                                dve.wait_ge(mm, n + 1)
                                nc.vector.tensor_copy(dst[:, h, hf * 512:(hf + 1) * 512], ps[n % 4][:, :])\
                                    .then_inc(copied, 1)
                                n += 1
                        dve.wait_ge(mm, n + 1)
                        src = ps[n % 4][:, 0:NT * H].rearrange("p (t h) -> p t h", h=H)
                        nc.vector.tensor_copy(s[:, :, :], src)
                        nc.vector.tensor_scalar(sa[:, :, :], src, SLOPE, None, ALU.mult).then_inc(copied, 1)

                r = ph.sb("r", [P, NT * H])
                block = ph.block()

                def finish(u, dve, link, o):
                    t, h = divmod(u, H)
                    link(nc.vector.reciprocal(r[:, u:u + 1], o[:, DH:DH + 1]))
                    return nc.vector.scalar_tensor_tensor(
                        out=x[:, t, h * DH:(h + 1) * DH], in0=o[:, 0:DH], scalar=r[:, u:u + 1],
                        in1=x[:, t, h * DH:(h + 1) * DH], op0=ALU.mult, op1=ALU.add)

                attention(block, ph, H, SLOPE, lambda u: False, lambda u: dst[:, u % H, :],
                          s[:, :, :].rearrange("p t h -> p (t h)"), sa[:, :, :].rearrange("p t h -> p (t h)"),
                          lambda u, c: V[:, c, u % H, :], DH + 1, finish, None, {})

        def graph2():
            KINDS = 3
            with Phase("g2") as ph:
                w = ph.sb("w", [P, DC, KINDS, D])
                HV = ph.sb("HV", [P, NT, KINDS, D])
                bias = ph.sb("bias", [P, D])
                adjT = [ph.sb(f"adjT{n}", [P, NT, P], I32) for n in range(2)]
                mask = [ph.sb(f"mask{n}", [P, KINDS, NT, P]) for n in range(2)]
                tps = [ph.ps(f"tps{n}", [P, DC, P]) for n in range(2)]
                psh = [ph.ps(f"psh{n}", [P, KINDS + 1, D]) for n in range(2)]
                pso = [ph.ps(f"pso{n}", [P, D]) for n in range(2)]
                loaded, vd, mm, copied = ph.sem("loaded"), ph.sem("vd"), ph.sem("mm"), ph.sem("copied")
                adjT_loaded = [ph.sem(f"adjT_loaded{n}") for n in range(2)]
                masked, summed, added = ph.sem("masked"), ph.sem("summed"), ph.sem("added")
                var_ready, rstd_ready = ph.sem("var_ready"), ph.sem("rstd_ready")
                xn_ready, tp_ready, xnT_ready = ph.sem("xn"), ph.sem("tp"), ph.sem("xnT")
                block = ph.block()
                adjT_v = A["adjT"].rearrange("(c p) i -> p c i", p=P)

                @block.sync
                def _(sp):
                    for v in range(KINDS):
                        sp.dma_start(w[:, :, v, :], A[f"L2_gnn_w{v + 1}"].rearrange("(c p) n -> p c n", p=P))\
                            .then_inc(loaded, 16)
                    sp.dma_start(bias[:, :], A["L2_gnn_bias"].unsqueeze(0).to_broadcast([P, D])).then_inc(loaded, 16)
                    for t in range(NT):
                        if t >= 2:
                            sp.wait_ge(masked, t - 1)
                        sp.dma_start(adjT[t % 2][:, :, :], adjT_v[:, :, t * P:(t + 1) * P])\
                            .then_inc(adjT_loaded[t % 2], 16)
                    sp.wait_ge(masked, NT)

                @block.tensor
                def _(pe):
                    norm_tensor(pe, tps, xn_ready, tp_ready, xnT_ready)
                    pe.wait_ge(loaded, 16 * (KINDS + 1))
                    for t in range(NT):
                        pe.wait_ge(xnT_ready, t + 1)
                        if t >= 2:
                            pe.wait_ge(copied, t - 1)
                        for v in range(KINDS):
                            for c in range(DC):
                                ins = nc.tensor.matmul(psh[t % 2][:, v, :], xnT[:, c, t * P:(t + 1) * P],
                                                       w[:, c, v, :], start=(c == 0), stop=(c == DC - 1))
                        ins.then_inc(mm, 1)
                    pe.wait_ge(copied, NT)
                    for t in range(NT):
                        pe.wait_ge(masked, t + 1)
                        if t >= 2:
                            pe.wait_ge(added, t - 1)
                        for v in range(KINDS):
                            for c in range(NT):
                                ins = nc.tensor.matmul(pso[t % 2][:, :], mask[t % 2][:, v, c, :], HV[:, c, v, :],
                                                       start=(v == 0 and c == 0), stop=(v == KINDS - 1 and c == NT - 1))
                        ins.then_inc(summed, 1)

                @block.gpsimd
                def _(pool):
                    norm_gpsimd(pool, var_ready, rstd_ready)

                @block.scalar
                def _(act):
                    norm_scalar(act, tps, tp_ready, xnT_ready)
                    for t in range(NT):
                        act.wait_ge(mm, t + 1)
                        nc.scalar.activation(HV[:, t, :, :], psh[t % 2][:, 0:KINDS, :], ACT.Copy).then_inc(copied, 1)

                @block.vector
                def _(dve):
                    link = linker(dve, vd)
                    norm_vector(dve, link, var_ready, rstd_ready, xn_ready)
                    dve.wait_ge(loaded, 16 * (KINDS + 1))
                    dve.wait_ge(xn_ready, NT)
                    link(nc.vector.tensor_tensor(x[:, :, :], x[:, :, :], bc(bias[:, :].unsqueeze(1), [P, NT, D]), ALU.add))

                    def masks(t):
                        dve.wait_ge(adjT_loaded[t % 2], 16 * (t // 2 + 1))
                        if t >= 2:
                            dve.wait_ge(summed, t - 1)
                        for v in range(KINDS):
                            ins = nc.vector.tensor_scalar(mask[t % 2][:, v, :, :], adjT[t % 2][:, :, :], float(v + 1),
                                                          None, ALU.is_equal)
                        ins.then_inc(masked, 1)

                    masks(0)
                    for t in range(NT):
                        if t + 1 < NT:
                            masks(t + 1)
                        dve.wait_ge(summed, t + 1)
                        nc.vector.tensor_tensor(x[:, t, :], x[:, t, :], pso[t % 2][:, :], ALU.add).then_inc(added, 1)

        def graph3():
            SLOPE = 0.2
            with Phase("g3") as ph:
                s = ph.sb("s", [P, NT, 2])
                sa = ph.sb("sa", [P, NT, 2])
                dst = ph.sb("dst", [P, 2, N])
                hp = ph.sb("hp", [P, NT, 2, D])
                with Phase("p3") as pp:
                    hT = pp.sb("hT", [P, DC, N])
                    w = pp.sb("w", [P, DC, D])
                    a = pp.sb("a", [P, 2, DC, 1])
                    a2b = pp.sb("a2b", [P, DC, P])
                    tps = [pp.ps(f"tps{n}", [P, DC, P]) for n in range(2)]
                    ps = [pp.ps(f"ps{n}", [P, 512]) for n in range(4)]
                    loaded = pp.sem("loaded")
                    var_ready, rstd_ready = pp.sem("var_ready"), pp.sem("rstd_ready")
                    xn_ready, tp_ready, xnT_ready = pp.sem("xn"), pp.sem("tp"), pp.sem("xnT")
                    vd, mm, copied, spread = pp.sem("vd"), pp.sem("mm"), pp.sem("copied"), pp.sem("spread")
                    blk = pp.block()

                    @blk.sync
                    def _(sp):
                        sp.dma_start(w[:, :, :], A["L3_gnn_W"].rearrange("(c p) n -> p c n", p=P)).then_inc(loaded, 16)
                        sp.dma_start(a[:, :, :, :].rearrange("p k c o -> p (k c o)"),
                                     A["L3_gnn_aT"]).then_inc(loaded, 16)
                        sp.wait_ge(loaded, 32)

                    @blk.tensor
                    def _(pe):
                        norm_tensor(pe, tps, xn_ready, tp_ready, xnT_ready)
                        pe.wait_ge(loaded, 32)
                        pe.wait_ge(xnT_ready, NT)
                        n = 0
                        for fc in range(DC):
                            for hf in range(2):
                                for c in range(DC):
                                    ins = nc.tensor.matmul(ps[n][:, :], w[:, c, fc * P:(fc + 1) * P],
                                                           xnT[:, c, hf * 512:(hf + 1) * 512],
                                                           start=(c == 0), stop=(c == DC - 1))
                                ins.then_inc(mm, 1)
                                n += 1
                        pe.wait_ge(spread, 1)
                        pe.wait_ge(copied, 4)
                        for hf in range(2):
                            for fc in range(DC):
                                ins = nc.tensor.matmul(ps[hf][:, :], a2b[:, fc, :], hT[:, fc, hf * 512:(hf + 1) * 512],
                                                       start=(fc == 0), stop=(fc == DC - 1))
                            ins.then_inc(mm, 1)
                        for t in range(NT):
                            for fc in range(DC):
                                ins = nc.tensor.matmul(ps[2][:, t:t + 1], hT[:, fc, t * P:(t + 1) * P], a[:, 0, fc, :],
                                                       start=(fc == 0), stop=(fc == DC - 1))
                        ins.then_inc(mm, 1)

                    @blk.gpsimd
                    def _(pool):
                        norm_gpsimd(pool, var_ready, rstd_ready)

                    @blk.scalar
                    def _(act):
                        norm_scalar(act, tps, tp_ready, xnT_ready)

                    @blk.vector
                    def _(dve):
                        link = linker(dve, vd)
                        norm_vector(dve, link, var_ready, rstd_ready, xn_ready)
                        dve.wait_ge(loaded, 32)
                        nc.vector.tensor_copy(a2b[:, :, :], bc(a[:, 1, :, :], [P, DC, P])).then_inc(spread, 1)
                        n = 0
                        for fc in range(DC):
                            for hf in range(2):
                                dve.wait_ge(mm, n + 1)
                                nc.vector.tensor_copy(hT[:, fc, hf * 512:(hf + 1) * 512], ps[n][:, :]).then_inc(copied, 1)
                                n += 1
                        for hf in range(2):
                            dve.wait_ge(mm, 5 + hf)
                            nc.vector.tensor_copy(dst[:, 0, hf * 512:(hf + 1) * 512], ps[hf][:, :])
                            nc.vector.tensor_scalar(dst[:, 1, hf * 512:(hf + 1) * 512], ps[hf][:, :], -1.0, None, ALU.mult)
                        dve.wait_ge(mm, 7)
                        for q, (o, f) in enumerate(((s, 1.0), (sa, SLOPE))):
                            for sign in range(2):
                                nc.vector.tensor_scalar(o[:, :, sign], ps[2][:, 0:NT], -f if sign else f, None, ALU.mult)

                r = ph.sb("r", [P, NT * 2])
                with Phase("a3") as pa:
                    block = pa.block()

                    def finish(u, dve, link, o):
                        t, sign = divmod(u, 2)
                        link(nc.vector.reciprocal(r[:, u:u + 1], o[:, D:D + 1]))
                        return nc.vector.tensor_scalar(hp[:, t, sign, :], o[:, 0:D], r[:, u:u + 1],
                                                       -1.0 if sign else 1.0, ALU.mult, ALU.mult)

                    attention(block, pa, 2, SLOPE, lambda u: u % 2 == 1, lambda u: dst[:, u % 2, :],
                              s[:, :, :].rearrange("p t h -> p (t h)"), sa[:, :, :].rearrange("p t h -> p (t h)"),
                              lambda u, c: xn[:, c, :], D + 1, finish, None, {})
                K4 = 2 * D // P
                wt = ph.sb("wt", [P, K4, D])
                hpT = ph.sb("hpT", [P, 2, K4, P])
                low, ex, z = ph.sb("low", [P, 2, D]), ph.sb("ex", [P, 2, D]), ph.sb("z", [P, 2, D])
                tp = [ph.ps(f"tp{n}", [P, K4, P]) for n in range(2)]
                pz = [ph.ps(f"pz{n}", [P, D]) for n in range(2)]
                loaded, turned, hpT_ready, mm = ph.sem("loaded"), ph.sem("turned"), ph.sem("hpT_ready"), ph.sem("mm")
                low_ready, ex_ready, done, vd = ph.sem("low_ready"), ph.sem("ex_ready"), ph.sem("done"), ph.sem("vd")
                block = ph.block()

                @block.sync
                def _(sp):
                    sp.dma_start(wt[:, :, :], A["L3_gnn_wtrans"].rearrange("(k p) n -> p k n", p=P)).then_inc(loaded, 16)
                    sp.wait_ge(loaded, 16)

                @block.tensor
                def _(pe):
                    def turn(t):
                        if t >= 2:
                            pe.wait_ge(hpT_ready, t - 1)
                        for k in range(K4):
                            ins = nc.tensor.transpose(tp[t % 2][:, k, :], hp[:, t, k // DC, k % DC * P:(k % DC + 1) * P],
                                                      ident[:, :])
                        ins.then_inc(turned, 1)
                    turn(0)
                    pe.wait_ge(loaded, 16)
                    for t in range(NT):
                        if t + 1 < NT:
                            turn(t + 1)
                        pe.wait_ge(hpT_ready, t + 1)
                        if t >= 2:
                            pe.wait_ge(done, t - 1)
                        for k in range(K4):
                            ins = nc.tensor.matmul(pz[t % 2][:, :], hpT[:, t % 2, k, :], wt[:, k, :],
                                                   start=(k == 0), stop=(k == K4 - 1))
                        ins.then_inc(mm, 1)

                @block.scalar
                def _(act):
                    for t in range(NT + 1):
                        if t < NT:
                            act.wait_ge(turned, t + 1)
                            if t >= 2:
                                act.wait_ge(mm, t - 1)
                            nc.scalar.activation(hpT[:, t % 2, :, :], tp[t % 2][:, :, :], ACT.Copy).then_inc(hpT_ready, 1)
                        if t >= 1:
                            act.wait_ge(low_ready, t)
                            nc.scalar.activation(ex[:, (t - 1) % 2, :], low[:, (t - 1) % 2, :], ACT.Exp)\
                                .then_inc(ex_ready, 1)

                @block.vector
                def _(dve):
                    link = linker(dve, vd)
                    for t in range(NT):
                        dve.wait_ge(mm, t + 1)
                        nc.vector.tensor_scalar(low[:, t % 2, :], pz[t % 2][:, :], 0.0, None, ALU.min).then_inc(low_ready, 1)
                        dve.wait_ge(ex_ready, t + 1)
                        link(nc.vector.scalar_tensor_tensor(out=z[:, t % 2, :], in0=pz[t % 2][:, :], scalar=0.0,
                                                            in1=ex[:, t % 2, :], op0=ALU.max, op1=ALU.add))
                        nc.vector.scalar_tensor_tensor(out=x[:, t, :], in0=z[:, t % 2, :], scalar=-1.0, in1=x[:, t, :],
                                                       op0=ALU.add, op1=ALU.add).then_inc(done, 1)

        def gate(L, E, gw_name, gb_name, all_probs, shared):
            T = max_tiles(E)
            with Phase(f"r{L}") as ph:
                gw = ph.sb("gw", [P, DC, E])
                gb = ph.sb("gb", [P, E])
                lg = ph.sb("lg", [P, NT, E])
                ez = ph.sb("ez", [P, NT, E])
                v8 = ph.sb("v8", [P, NT, 8])
                i8 = ph.sb("i8", [P, NT, 8], U32)
                idx = ph.sb("idx", [P, NT, 2])
                oh = ph.sb("oh", [P, 2, NT, E])
                both = ph.sb("both", [P, NT, E], BF16)
                cnt = ph.sb("cnt", [P, E, 1])
                over = ph.sb("over", [P, E, NT])
                tiles = ph.sb("tiles", [P, E])
                prev = ph.sb("prev", [P, E, E])
                base = ph.sb("base", [P, E])
                upto = ph.sb("upto", [P, E])
                rank = ph.sb("rank", [P, NT, E])
                prod = ph.sb("prod", [P, 2, NT, E])
                posf = ph.sb("posf", [P, 2, NT])
                past = ph.sb("past", [1, T, E])
                et = ph.sb("et", [1, T])
                den = ph.sb("den", [P, 3, NT])
                tps = [ph.ps(f"tps{n}", [P, DC, P]) for n in range(2)]
                psl = ph.ps("psl", [P, NT, E])
                psr = ph.ps("psr", [P, NT, E])
                psc = ph.ps("psc", [P, E])
                loaded, vd, mm, exped = ph.sem("loaded"), ph.sem("vd"), ph.sem("mm"), ph.sem("exped")
                onehot, placed, centred = ph.sem("onehot"), ph.sem("placed"), ph.sem("centred")
                scattered, shared_placed = ph.sem("scattered"), ph.sem("shared_placed")
                var_ready, rstd_ready = ph.sem("var_ready"), ph.sem("rstd_ready")
                xn_ready, tp_ready, xnT_ready = ph.sem("xn"), ph.sem("tp"), ph.sem("xnT")
                block = ph.block()
                ALL = 32 if gb_name else 16

                @block.sync
                def _(sp):
                    sp.dma_start(gw[:, :, :], A[gw_name].rearrange("(c p) n -> p c n", p=P)).then_inc(loaded, 16)
                    if gb_name:
                        sp.dma_start(gb[:, :], A[gb_name].unsqueeze(0).to_broadcast([P, E])).then_inc(loaded, 16)
                    if shared:
                        sp.wait_ge(xn_ready, NT)
                        sp.dma_start(x_slots[T * P:(T + NT) * P, :].rearrange("(t p) d -> p t d", p=P),
                                     xn[:, :, 0:D]).then_inc(shared_placed, 16)
                        sp.wait_ge(shared_placed, 16)
                    sp.wait_ge(scattered, 16 * 2 * NT)

                @block.tensor
                def _(pe):
                    norm_tensor(pe, tps, xn_ready, tp_ready, xnT_ready)
                    pe.wait_ge(loaded, ALL)
                    pe.wait_ge(xnT_ready, NT)
                    for t in range(NT):
                        for c in range(DC):
                            ins = nc.tensor.matmul(psl[:, t, :], xnT[:, c, t * P:(t + 1) * P], gw[:, c, :],
                                                   start=(c == 0), stop=(c == DC - 1))
                    ins.then_inc(mm, 1)
                    pe.wait_ge(onehot, 1)
                    for t in range(NT):
                        for q in range(t + 1):
                            nc.tensor.matmul(psr[:, t, :], (before_b if q == t else ones_b)[:, :], both[:, q, :],
                                             start=(q == 0), stop=(q == t))
                    for q in range(NT):
                        ins = nc.tensor.matmul(psc[:, :], ones_b[:, :], both[:, q, :], start=(q == 0), stop=(q == NT - 1))
                    ins.then_inc(mm, 1)

                @block.scalar
                def _(act):
                    norm_scalar(act, tps, tp_ready, xnT_ready)
                    act.wait_ge(centred, 1)
                    nc.scalar.activation(ez[:, :, :], ez[:, :, :], ACT.Exp)
                    nc.scalar.activation(den[:, 0, :], den[:, 0, :], ACT.Exp).then_inc(exped, 1)

                @block.vector
                def _(dve):
                    link = linker(dve, vd)
                    norm_vector(dve, link, var_ready, rstd_ready, xn_ready)
                    dve.wait_ge(mm, 1)
                    dve.wait_ge(loaded, ALL)
                    if gb_name:
                        link(nc.vector.tensor_tensor(lg[:, :, :], psl[:, :, :], bc(gb[:, :].unsqueeze(1), [P, NT, E]),
                                                     ALU.add))
                    else:
                        link(nc.vector.tensor_copy(lg[:, :, :], psl[:, :, :]))
                    for t in range(NT):
                        ins = nc.vector.max(out=v8[:, t, :], in_=lg[:, t, :])
                    link(ins)
                    nc.vector.tensor_tensor(ez[:, :, :], lg[:, :, :], bc(v8[:, :, 0:1], [P, NT, E]), ALU.subtract)
                    nc.vector.tensor_tensor(den[:, 0, :], v8[:, :, 1], v8[:, :, 0], ALU.subtract).then_inc(centred, 1)
                    for t in range(NT):
                        ins = nc.vector.max_index(out=i8[:, t, :], in_max=v8[:, t, :], in_values=lg[:, t, :])
                    link(ins)
                    link(nc.vector.tensor_copy(idx[:, :, :], i8[:, :, 0:2]))
                    for k in range(2):
                        ins = nc.vector.tensor_tensor(oh[:, k, :, :], bc(iota_f[:, 0:E].unsqueeze(1), [P, NT, E]),
                                                      bc(idx[:, :, k:k + 1], [P, NT, E]), ALU.is_equal)
                    link(ins)
                    nc.vector.tensor_tensor(both[:, :, :], oh[:, 0, :, :], oh[:, 1, :, :], ALU.add).then_inc(onehot, 1)
                    dve.wait_ge(exped, 1)
                    if all_probs:
                        link(nc.vector.tensor_reduce(den[:, 1, :], ez[:, :, :], AX.X, ALU.add))
                    else:
                        link(nc.vector.tensor_scalar(den[:, 1, :], den[:, 0, :], 1.0, None, ALU.add))
                    link(nc.vector.reciprocal(wts[:, 0, :], den[:, 1, :]))
                    nc.vector.tensor_tensor(wts[:, 1, :], den[:, 0, :], wts[:, 0, :], ALU.mult)
                    dve.wait_ge(mm, 2)
                    link(nc.vector.tensor_copy(cnt[:, :, 0], psc[:, :]))
                    link(nc.vector.tensor_tensor(over[:, :, :], bc(cnt[:, :, :], [P, E, NT]),
                                                 bc(iota_128[:, :].unsqueeze(1), [P, E, NT]), ALU.is_gt))
                    link(nc.vector.tensor_reduce(tiles[:, :], over[:, :, :], AX.X, ALU.add))
                    link(nc.vector.tensor_tensor(prev[:, :, :], bc(tiles[:, :].unsqueeze(1), [P, E, E]),
                                                 before_e[:, 0:E, 0:E], ALU.mult))
                    link(nc.vector.tensor_reduce(base[:, :], prev[:, :, :], AX.X, ALU.add))
                    nc.vector.tensor_tensor(upto[:, :], base[:, :], tiles[:, :], ALU.add)
                    link(nc.vector.scalar_tensor_tensor(out=rank[:, :, :], in0=bc(base[:, :].unsqueeze(1), [P, NT, E]),
                                                        scalar=float(P), in1=psr[:, :, :], op0=ALU.mult, op1=ALU.add))
                    for k in range(2):
                        ins = nc.vector.tensor_tensor(prod[:, k, :, :], oh[:, k, :, :], rank[:, :, :], ALU.mult)
                    link(ins)
                    link(nc.vector.tensor_reduce(posf[:, :, :], prod[:, :, :, :], AX.X, ALU.add))
                    nc.vector.tensor_copy(pos[:, :, :], posf[:, :, :]).then_inc(placed, 1)
                    link(nc.vector.tensor_tensor(past[:, :, :], bc(upto[0:1, :].unsqueeze(1), [1, T, E]),
                                                 bc(iota_f[0:1, 0:T].unsqueeze(2), [1, T, E]), ALU.is_le))
                    link(nc.vector.tensor_reduce(et[:, :], past[:, :, :], AX.X, ALU.add))
                    if shared:
                        nc.vector.memset(etab[0:1, T:T + NT], E)
                    link(nc.vector.tensor_scalar(etab[0:1, 0:T], et[:, :], float(E - 1), None, ALU.min))

                @block.gpsimd
                def _(pool):
                    norm_gpsimd(pool, var_ready, rstd_ready)
                    pool.wait_ge(placed, 1)
                    for t in range(NT):
                        for k in range(2):
                            pool.indirect_dma_start(
                                out=x_slots[:, :], out_offset=bass.IndirectOffsetOnAxis(ap=pos[:, k, t:t + 1], axis=0),
                                in_=xn[:, t, 0:D], in_offset=None).then_inc(scattered, 16)

        def experts(L, E, F, kind, shared, w1_name, w2_name, b2_name):
            T = max_tiles(E) + (NT if shared else 0)
            EN = E + shared
            FC = F // P
            up = 2 if kind == "silu" else 1
            W1C = up * DC * F + (0 if kind == "silu" else FC)
            FULL = (T - 2) // UN
            with Phase(f"e{L}") as ph:
                w1 = [ph.sb(f"w1{n}", [P, W1C]) for n in range(UN)]
                w2 = [ph.sb(f"w2{n}", [P, FC * D]) for n in range(UN)]
                b2 = [ph.sb(f"b2{n}", [P, D]) for n in range(UN)] if b2_name else None
                xs = [ph.sb(f"xs{n}", [P, D]) for n in range(UN)]
                ys = [ph.sb(f"ys{n}", [P, D]) for n in range(UN)]
                xsT = [ph.sb(f"xsT{n}", [P, DC, P]) for n in range(2)]
                hT = [ph.sb(f"hT{n}", [P, FC, P]) for n in range(2)]
                sg = [ph.sb(f"sg{n}", [P, FC, P]) for n in range(2)] if kind == "silu" else None
                pT = [ph.ps(f"pT{n}", [P, DC, P]) for n in range(2)]
                pH = [ph.ps(f"pH{n}", [P, up * FC, P]) for n in range(2)]
                pY = [ph.ps(f"pY{n}", [P, D]) for n in range(2)]
                xs_loaded = [ph.sem(f"xs_loaded{n}") for n in range(UN)]
                w1_loaded = [ph.sem(f"w1_loaded{n}") for n in range(UN)]
                w2_loaded = [ph.sem(f"w2_loaded{n}") for n in range(UN)]
                y_stored = [ph.sem(f"y_stored{n}") for n in range(UN)]
                turned, xsT_ready = ph.sem("turned"), ph.sem("xsT_ready")
                h_summed, h_gated, h_ready = ph.sem("h_summed"), ph.sem("h_gated"), ph.sem("h_ready")
                y_summed, y_ready = ph.sem("y_summed"), ph.sem("y_ready")
                block = ph.block()
                w1_v, w2_v = A[w1_name], A[w2_name]
                W2_INC = 32 if b2_name else 16

                def loop(eng, step):
                    for b in range(UN):
                        step(0, b)
                    with eng.Fori(1, FULL) as i:
                        for b in range(UN):
                            step(i, b)
                    for t in range(UN * FULL, T):
                        step(t // UN, t % UN)

                def later(i, b, by):
                    return i + (b + by) // UN, (b + by) % UN

                def first(i, b, before):
                    return isinstance(i, int) and UN * i + b < before

                def last(i, b):
                    return isinstance(i, int) and UN * i + b >= T

                @block.sync
                def _(sp):
                    def store(i, b):
                        t = UN * i + b
                        sp.dma_start(y_slots[bass.ds(t * P, P), :], ys[b][:, :]).then_inc(y_stored[b], 16)

                    def step(i, b):
                        t = UN * i + b
                        if not first(i, b, UN):
                            sp.wait_ge(y_ready, t - UN + 1)
                        e = sp.value_load(etab[0:1, bass.ds(t, 1)], min_val=0, max_val=EN - 1)
                        sp.dma_start(xs[b][:, :], x_slots[bass.ds(t * P, P), :]).then_inc(xs_loaded[b], 16)
                        sp.dma_start(w1[b][:, :], w1_v[bass.ds(e, 1), :, :].rearrange("a p c -> (a p) c"))\
                            .then_inc(w1_loaded[b], 16)
                        sp.dma_start(w2[b][:, :], w2_v[bass.ds(e, 1), :, :].rearrange("a p c -> (a p) c"))\
                            .then_inc(w2_loaded[b], 16)
                        if b2_name:
                            sp.dma_start(b2[b][:, :], A[b2_name][bass.ds(e, 1), :].to_broadcast([P, D]))\
                                .then_inc(w2_loaded[b], 16)
                        if not first(i, b, UN):
                            store(i - 1, b)
                    loop(sp, step)
                    for t in range(T - UN, T):
                        sp.wait_ge(y_ready, t + 1)
                        store(t // UN, t % UN)
                    for b in range(UN):
                        sp.wait_ge(y_stored[b], 16 * len(range(b, T, UN)))

                @block.tensor
                def _(pe):
                    def turn(i, b):
                        t = UN * i + b
                        pe.wait_ge(xs_loaded[b], 16 * (i + 1))
                        if not first(i, b, 2):
                            pe.wait_ge(xsT_ready, t - 1)
                        for c in range(DC):
                            ins = nc.tensor.transpose(pT[b % 2][:, c, :], xs[b][:, c * P:(c + 1) * P], ident[:, :])
                        ins.then_inc(turned, 1)

                    def rise(i, b):
                        t = UN * i + b
                        pe.wait_ge(w1_loaded[b], 16 * (i + 1))
                        pe.wait_ge(xsT_ready, t + 1)
                        if not first(i, b, 2):
                            pe.wait_ge(h_ready, t - 1)
                        for f in range(up * FC):
                            for c in range(DC):
                                at = (f // FC * DC + c) * F + f % FC * P
                                ins = nc.tensor.matmul(pH[b % 2][:, f, :], w1[b][:, at:at + P], xsT[b % 2][:, c, :],
                                                       start=(c == 0), stop=(c == DC - 1))
                        ins.then_inc(h_summed, 1)

                    def fall(i, b):
                        t = UN * i + b
                        pe.wait_ge(w2_loaded[b], W2_INC * (i + 1))
                        pe.wait_ge(h_ready, t + 1)
                        if not first(i, b, 2):
                            pe.wait_ge(y_ready, t - 1)
                        for f in range(FC):
                            ins = nc.tensor.matmul(pY[b % 2][:, :], hT[b % 2][:, f, :], w2[b][:, f * D:(f + 1) * D],
                                                   start=(f == 0), stop=(f == FC - 1))
                        ins.then_inc(y_summed, 1)

                    turn(0, 0)
                    turn(0, 1)
                    rise(0, 0)

                    def step(i, b):
                        if not last(*later(i, b, 2)):
                            turn(*later(i, b, 2))
                        if not last(*later(i, b, 1)):
                            rise(*later(i, b, 1))
                        fall(i, b)
                    loop(pe, step)

                @block.scalar
                def _(act):
                    def step(i, b):
                        t = UN * i + b
                        act.wait_ge(h_summed, t + 1)
                        if kind == "silu":
                            if not first(i, b, 2):
                                act.wait_ge(h_ready, t - 1)
                            nc.scalar.activation(sg[b % 2][:, :, :], pH[b % 2][:, 0:FC, :], ACT.Silu)\
                                .then_inc(h_gated, 1)
                            return
                        if not first(i, b, 2):
                            act.wait_ge(y_summed, t - 1)
                        for f in range(FC):
                            b1 = w1[b][:, DC * F + f:DC * F + f + 1]
                            ins = nc.scalar.activation(hT[b % 2][:, f, :], pH[b % 2][:, f, :],
                                                       ACT.Relu if kind == "relu" else ACT.Gelu, bias=b1)
                        ins.then_inc(h_ready, 1)
                    loop(act, step)

                @block.vector
                def _(dve):
                    def copy(i, b):
                        t = UN * i + b
                        dve.wait_ge(turned, t + 1)
                        if not first(i, b, 2):
                            dve.wait_ge(h_summed, t - 1)
                        nc.vector.tensor_copy(xsT[b % 2][:, :, :], pT[b % 2][:, :, :]).then_inc(xsT_ready, 1)

                    def product(i, b):
                        t = UN * i + b
                        dve.wait_ge(h_gated, t + 1)
                        if not first(i, b, 2):
                            dve.wait_ge(y_summed, t - 1)
                        nc.vector.tensor_tensor(hT[b % 2][:, :, :], sg[b % 2][:, :, :], pH[b % 2][:, FC:2 * FC, :],
                                                ALU.mult).then_inc(h_ready, 1)

                    def end(i, b):
                        t = UN * i + b
                        dve.wait_ge(y_summed, t + 1)
                        if not first(i, b, UN):
                            dve.wait_ge(y_stored[b], 16 * i)
                        if b2_name:
                            ins = nc.vector.tensor_tensor(ys[b][:, :], pY[b % 2][:, :], b2[b][:, :], ALU.add)
                        else:
                            ins = nc.vector.tensor_copy(ys[b][:, :], pY[b % 2][:, :])
                        ins.then_inc(y_ready, 1)

                    copy(0, 0)
                    copy(0, 1)
                    if kind == "silu":
                        product(0, 0)

                    def step(i, b):
                        if not last(*later(i, b, 2)):
                            copy(*later(i, b, 2))
                        if kind == "silu" and not last(*later(i, b, 1)):
                            product(*later(i, b, 1))
                        end(i, b)
                    loop(dve, step)

        def combine(L, E, shared, post_norm, final):
            T = max_tiles(E)
            with Phase(f"c{L}") as ph:
                yg = ph.sb("yg", [P, NT, 2, D])
                ysh = ph.sb("ysh", [P, NT, D]) if shared else None
                gathered = [ph.sem(f"gathered{t}") for t in range(NT)]
                var_ready, rstd_ready = ph.sem("var_ready"), ph.sem("rstd_ready")
                loaded, vd, stored, ready = ph.sem("loaded"), ph.sem("vd"), ph.sem("stored"), ph.sem("ready")
                if post_norm:
                    z = ph.sb("z", [P, NT, D])
                    gamma, beta = ph.sb("gamma", [P, D]), ph.sb("beta", [P, D])
                block = ph.block()
                loads = []
                if post_norm:
                    loads += [(gamma[:, :], A["L0_ffn_gamma"].unsqueeze(0).to_broadcast([P, D])),
                              (beta[:, :], A["L0_ffn_beta"].unsqueeze(0).to_broadcast([P, D]))]
                if shared:
                    loads += [(ysh[:, :, :], y_slots[T * P:(T + NT) * P, :].rearrange("(t p) d -> p t d", p=P))]
                ALL = 16 * len(loads)

                @block.sync
                def _(sp):
                    for dst, src in loads:
                        sp.dma_start(dst, src).then_inc(loaded, 16)
                    if loads:
                        sp.wait_ge(loaded, ALL)
                    if final:
                        o_v = out.rearrange("(t p) d -> p t d", p=P)
                        for t in range(NT):
                            sp.wait_ge(ready, t + 1)
                            sp.dma_start(o_v[:, t, :], x[:, t, :]).then_inc(stored, 16)
                        sp.wait_ge(stored, 16 * NT)

                @block.gpsimd
                def _(pool):
                    for t in range(NT):
                        for k in range(2):
                            pool.indirect_dma_start(
                                out=yg[:, t, k, :], out_offset=None, in_=y_slots[:, :],
                                in_offset=bass.IndirectOffsetOnAxis(ap=pos[:, k, t:t + 1], axis=0))\
                                .then_inc(gathered[t], 16)
                    if post_norm:
                        norm_gpsimd(pool, var_ready, rstd_ready)

                @block.vector
                def _(dve):
                    link = linker(dve, vd)
                    if loads:
                        dve.wait_ge(loaded, ALL)
                    for t in range(NT):
                        acc = z[:, t, :] if post_norm else x[:, t, :]
                        if shared:
                            link(nc.vector.tensor_tensor(acc, acc, ysh[:, t, :], ALU.add))
                        dve.wait_ge(gathered[t], 32)
                        link(nc.vector.scalar_tensor_tensor(
                            out=acc, in0=yg[:, t, 0, :], scalar=wts[:, 0, t:t + 1],
                            in1=xn[:, t, 0:D] if post_norm else acc, op0=ALU.mult, op1=ALU.add))
                        nc.vector.scalar_tensor_tensor(out=acc, in0=yg[:, t, 1, :], scalar=wts[:, 1, t:t + 1],
                                                       in1=acc, op0=ALU.mult, op1=ALU.add).then_inc(ready, 1)
                    if post_norm:
                        dve.wait_ge(ready, NT)
                        for t in range(NT):
                            ins = nc.vector.bn_stats(out=stats[:, t, :], in_=z[:, t, :])
                        link(ins)
                        for t in range(NT):
                            ins = nc.vector.bn_aggr(out=mean_var[:, t, :], in_=stats[:, t, :])
                        ins.then_inc(var_ready, 1)
                        dve.wait_ge(rstd_ready, 2)
                        for t in range(NT):
                            ins = nc.vector.tensor_scalar(z[:, t, :], z[:, t, :], mean_var[:, t, 0:1], rstd[:, t, :],
                                                          ALU.subtract, ALU.mult)
                        link(ins)
                        link(nc.vector.tensor_tensor(z[:, :, :], z[:, :, :], bc(gamma[:, :].unsqueeze(1), [P, NT, D]),
                                                     ALU.mult))
                        link(nc.vector.tensor_tensor(z[:, :, :], z[:, :, :], bc(beta[:, :].unsqueeze(1), [P, NT, D]),
                                                     ALU.add))
                        nc.vector.tensor_tensor(x[:, :, :], x[:, :, :], z[:, :, :], ALU.add)

        def early_out():
            with Phase("early") as ph:
                stored = ph.sem("stored")
                block = ph.block()

                @block.sync
                def _(sp):
                    sp.dma_start(out.rearrange("(t p) d -> p t d", p=P), x[:, :, :]).then_inc(stored, 16)
                    sp.wait_ge(stored, 16)

        def ffn(L, E, F, kind, gw, gb, b2=True, all_probs=False, shared=0, post_norm=False, final=False):
            gate(L, E, gw, gb, all_probs, shared)
            experts(L, E, F, kind, shared, f"w1_{L}", f"w2_{L}", f"b2_{L}" if b2 else None)
            combine(L, E, shared, post_norm, final)

        halves = [graph0,
                  lambda: ffn(0, 16, 512, "relu", "L0_ffn_gate_w", "L0_ffn_gate_b", post_norm=True),
                  graph1,
                  lambda: ffn(1, 8, 512, "gelu", "L1_ffn_gate_w", "L1_ffn_gate_b", all_probs=True),
                  graph2,
                  lambda: ffn(2, 8, 1024, "gelu", "L2_ffn_Wr", None, shared=1),
                  graph3,
                  lambda: ffn(3, 16, 512, "silu", "L3_ffn_gate_w", "L3_ffn_gate_b", b2=False, final=True)]
        for n, half in enumerate(halves[:stop]):
            half()
            if n % 2 == 1:
                nc.clear_and_free_semaphores(sems)
                sems.clear()
                nc.all_engine_barrier()
        if stop < len(halves):
            early_out()


def _arrays(inputs):
    import numpy as np

    def a(n):
        return np.asarray(inputs[n])

    def rows(w):
        e, k, f = w.shape
        return w.reshape(e, k // P, P, f).transpose(0, 2, 1, 3).reshape(e, P, k // P * f)

    def cols(b):
        return b.reshape(b.shape[0], -1, P).transpose(0, 2, 1)

    out = {n: a(n) for n in inputs if not n.split("_", 1)[-1].startswith("ffn")}
    for n in ("L0_ffn_gate_w", "L0_ffn_gate_b", "L0_ffn_gamma", "L0_ffn_beta", "L1_ffn_gate_w", "L1_ffn_gate_b",
              "L2_ffn_Wr", "L3_ffn_gate_w", "L3_ffn_gate_b"):
        out[n] = a(n)
    out["adjT"] = a("adj").T
    out["neighT"] = out.pop("L0_gnn_neigh").T
    out["L1_gnn_WT"] = out.pop("L1_gnn_W").T
    out["L3_gnn_aT"] = out.pop("L3_gnn_a").reshape(-1, P).T
    out["w1_0"] = np.concatenate([rows(a("L0_ffn_w1")), cols(a("L0_ffn_b1"))], 2)
    out["w2_0"], out["b2_0"] = rows(a("L0_ffn_w2")), a("L0_ffn_b2")
    out["w1_1"] = np.concatenate([rows(a("L1_ffn_W1")), cols(a("L1_ffn_b1"))], 2)
    out["w2_1"], out["b2_1"] = rows(a("L1_ffn_W2")), a("L1_ffn_b2")
    w1 = np.concatenate([a("L2_ffn_W1p"), a("L2_ffn_W1s")[None]])
    w2 = np.concatenate([a("L2_ffn_W2p"), a("L2_ffn_W2s")[None]])
    out["w1_2"] = np.concatenate([rows(w1), cols(np.concatenate([a("L2_ffn_b1p"), a("L2_ffn_b1s")[None]]))], 2)
    out["w2_2"], out["b2_2"] = rows(w2), np.concatenate([a("L2_ffn_b2p"), a("L2_ffn_b2s")[None]])
    out["w1_3"] = np.concatenate([rows(a("L3_ffn_w1")), rows(a("L3_ffn_w2"))], 2)
    out["w2_3"] = rows(a("L3_ffn_w3"))
    return {n: np.ascontiguousarray(v) for n, v in out.items()}


STOP = 99


def kernel(**inputs):
    import numpy as np
    import concourse.bacc as bacc
    from concourse.bass_utils import run_bass_kernel_spmd

    nc = bacc.Bacc("TRN2", target_bir_lowering=False, num_devices=1)
    arrays = _arrays(inputs)
    A = {n: nc.dram_tensor(n + "_in", v.shape, mybir.dt.from_np(v.dtype), kind="ExternalInput").ap()
         for n, v in arrays.items()}
    out = nc.dram_tensor("out", [N, D], mybir.dt.float32, kind="ExternalOutput").ap()
    build(nc, A, out, STOP)
    r = run_bass_kernel_spmd(nc, [{n + "_in": v for n, v in arrays.items()}], core_ids=[0])
    return np.asarray(r.results[0]["out"])
```

```python
import concourse.bass as bass
from concourse import mybir
from contextlib import ExitStack

P = 128
N = 1024
NT = N // P
D = 256
DC = D // P
EPS = 1e-5
MASKED = -1e30
UN = 4


def build(nc, A, out, stop=99):
    F32, BF16, I32, U32 = mybir.dt.float32, mybir.dt.bfloat16, mybir.dt.int32, mybir.dt.uint32
    F32R = mybir.dt.float32r
    ALU, ACT, AX = mybir.AluOpType, mybir.ActivationFunctionType, mybir.AxisListType

    def max_tiles(experts):
        return (2 * N + experts * (P - 1)) // P

    def loop_tiles(experts, first):
        return -(-(first + max_tiles(experts)) // UN) * UN

    SLOTS = max(loop_tiles(16, 0), loop_tiles(8, NT)) * P
    xn_rows = nc.dram_tensor("xn_rows", [N, D], F32, kind="Internal").ap()
    OWN = 2 * N
    y_rows = nc.dram_tensor("y_rows", [OWN + SLOTS, D], F32, kind="Internal").ap()

    top = ExitStack()
    with top:
        def keep(name, shape, dt=F32):
            return top.enter_context(nc.sbuf_tensor(name, shape, dt))

        x = keep("x", [P, NT, D])
        xn = keep("xn", [P, NT, D + 1])
        xnT = keep("xnT", [P, DC, N])
        neg = keep("neg", [P, NT, N])
        ident = keep("ident", [P, P])
        ones_b = keep("ones_b", [P, P], BF16)
        before_b = keep("before_b", [P, P], BF16)
        iota_128 = keep("iota_128", [P, NT])
        iota_un = keep("iota_un", [P, NT])
        before_e = keep("before_e", [P, 16, 16])
        stats = keep("stats", [P, NT, 6])
        mean_var = keep("mean_var", [P, NT, 2])
        rstd = keep("rstd", [P, NT, 1])
        power = keep("power", [P, NT, 1])
        wts = keep("wts", [P, 2, NT])
        etab = keep("etab", [1, 32], I32)
        more = keep("more", [1, 1], I32)
        table = keep("table", [P, 32], U32)
        dest = keep("dest", [P, 32], U32)
        own = keep("own", [P, 32])
        iota_row = keep("iota_row", [P, P])
        iota_p = keep("iota_p", [P, 1])
        pair_row = keep("pair_row", [P, 2, NT])

        sems = []

        class Phase:

            def __init__(self, name):
                self.name, self.ctx = name, ExitStack()

            def __enter__(self):
                return self

            def sb(self, name, shape, dt=F32):
                return self.ctx.enter_context(nc.sbuf_tensor(f"{self.name}_{name}", shape, dt))

            def ps(self, name, shape, dt=F32):
                return self.ctx.enter_context(nc.psum_tensor(f"{self.name}_{name}", shape, dt))

            def sem(self, name):
                sems.append(nc.alloc_semaphore(f"{self.name}_{name}"))
                return sems[-1]

            def block(self):
                return self.ctx.enter_context(nc.Block(no_gpsimd_drain=True))

            def __exit__(self, *a):
                return self.ctx.__exit__(*a)

        def linker(eng, sem):
            count = [0]

            def link(ins):
                count[0] += 1
                ins.then_inc(sem, 1)
                eng.wait_ge(sem, count[0])
            return link

        def bc(ap, shape):
            return ap.to_broadcast(shape)

        def norm_gpsimd(pool, var_ready, rstd_ready):
            pool.wait_ge(var_ready, 1)
            nc.gpsimd.tensor_scalar(mean_var[:, :, 1:2], mean_var[:, :, 1:2], EPS, None, ALU.add)\
                .then_inc(rstd_ready, 1)
            pool.wait_ge(rstd_ready, 1)
            nc.gpsimd.tensor_tensor(rstd[:, :, :], mean_var[:, :, 1:2], power[:, :, :], ALU.pow)\
                .then_inc(rstd_ready, 1)

        def norm_vector(dve, link, var_ready, rstd_ready, xn_ready):
            for t in range(NT):
                ins = nc.vector.bn_stats(out=stats[:, t, :], in_=x[:, t, :])
            link(ins)
            for t in range(NT):
                ins = nc.vector.bn_aggr(out=mean_var[:, t, :], in_=stats[:, t, :])
            ins.then_inc(var_ready, 1)
            dve.wait_ge(rstd_ready, 2)
            for t in range(NT):
                nc.vector.tensor_scalar(xn[:, t, 0:D], x[:, t, :], mean_var[:, t, 0:1], rstd[:, t, :],
                                        ALU.subtract, ALU.mult).then_inc(xn_ready, 1)

        def norm_tensor(pe, tps, xn_ready, tp_ready, xnT_ready):
            for t in range(NT):
                pe.wait_ge(xn_ready, t + 1)
                if t >= 2:
                    pe.wait_ge(xnT_ready, t - 1)
                for c in range(DC):
                    ins = nc.tensor.transpose(tps[t % 2][:, c, :], xn[:, t, c * P:(c + 1) * P], ident[:, :])
                ins.then_inc(tp_ready, 1)

        def norm_scalar(act, tps, tp_ready, xnT_ready):
            for t in range(NT):
                act.wait_ge(tp_ready, t + 1)
                nc.scalar.activation(xnT[:, :, t * P:(t + 1) * P], tps[t % len(tps)][:, :, :], ACT.Copy)\
                    .then_inc(xnT_ready, 1)

        def constants(ph, neighT, neigh_loaded):
            iota_i = ph.sb("iota_i", [P, P], I32)
            iota_pi = ph.sb("iota_pi", [P, 1], I32)
            loaded, made, made_v = ph.sem("loaded"), ph.sem("made"), ph.sem("made_v")
            block = ph.block()

            @block.sync
            def _(sp):
                sp.dma_start(x[:, :, :], A["x"].rearrange("(t p) d -> p t d", p=P)).then_inc(loaded, 16)
                sp.dma_start(neighT[:, :, :], A["neighT"].rearrange("(c p) n -> p c n", p=P))\
                    .then_inc(neigh_loaded, 16)
                sp.wait_ge(loaded, 16)

            @block.gpsimd
            def _(pool):
                link = linker(pool, made)
                link(nc.gpsimd.memset(ident[:, :], 0.0))
                nc.gpsimd.affine_select(out=ident[:, :], in_=ident[:, :], compare_op=ALU.not_equal, fill=1.0,
                                        base=0, pattern=[[-1, P]], channel_multiplier=1)
                link(nc.gpsimd.memset(before_b[:, :], 1.0))
                nc.gpsimd.affine_select(out=before_b[:, :], in_=before_b[:, :], compare_op=ALU.is_gt, fill=0.0,
                                        base=0, pattern=[[1, P]], channel_multiplier=-1)
                nc.gpsimd.iota(iota_i[:, :], pattern=[[1, P]], base=0, channel_multiplier=0)
                link(nc.gpsimd.iota(iota_pi[:, :], pattern=[[1, 1]], base=0, channel_multiplier=1))

            @block.vector
            def _(dve):
                link = linker(dve, made_v)
                nc.vector.memset(ones_b[:, :], 1.0)
                nc.vector.memset(power[:, :, :], -0.5)
                nc.vector.memset(xn[:, :, D:D + 1], 1.0)
                dve.wait_ge(made, 3)
                nc.vector.tensor_copy(iota_p[:, :], iota_pi[:, :])
                link(nc.vector.tensor_copy(iota_row[:, :], iota_i[:, :]))
                nc.vector.tensor_scalar(pair_row[:, :, :].rearrange("p k t -> p (k t)"), iota_row[:, 0:2 * NT], 1.0, None,
                                        ALU.add)
                link(nc.vector.tensor_scalar(own[:, :], iota_row[:, 0:32], float(P), float(OWN), ALU.mult, ALU.add))
                nc.vector.tensor_scalar(own[:, :], own[:, :], iota_p[:, :], None, ALU.add)
                nc.vector.tensor_scalar(iota_128[:, :], iota_row[:, 0:NT], float(P), None, ALU.mult)
                nc.vector.tensor_scalar(iota_un[:, :], iota_row[:, 0:NT], float(UN), None, ALU.mult)
                nc.vector.tensor_tensor(before_e[:, :, :], bc(iota_row[:, 0:16].unsqueeze(1), [P, 16, 16]),
                                        bc(iota_row[:, 0:16].unsqueeze(2), [P, 16, 16]), ALU.is_lt)

        def attention(block, ph, heads, slope, lowest, rows, s, sa, values, width, finish,
                      scores=None, extra=()):
            units = NT * heads
            g = [ph.sb(f"g{n}", [P, N]) for n in range(4)]
            t2 = [ph.sb(f"t2{n}", [P, N]) for n in range(4)]
            lm = [ph.sb(f"lm{n}", [P, N]) for n in range(2)]
            pT = [ph.sb(f"pT{n}", [P, NT, P]) for n in range(2)]
            small = ph.sb("small", [P, 6, units])
            gm, y, ay, m, b1, b2 = (small[:, n, :] for n in range(6))
            tp = [ph.ps(f"tp{n}", [P, NT, P]) for n in range(2)]
            o = [ph.ps(f"o{n}", [P, 512]) for n in range(2)]
            scored, maxed, biased = ph.sem("scored"), ph.sem("maxed"), ph.sem("biased")
            sloped, shifted, turned = ph.sem("sloped"), ph.sem("shifted"), ph.sem("turned")
            exped, weighed, finished = ph.sem("exped"), ph.sem("weighed"), ph.sem("finished")
            pool_done, vec_done = ph.sem("pool_done"), ph.sem("vec_done")

            @block.vector
            def _(dve):
                link = linker(dve, vec_done)
                if "vector" in extra:
                    extra["vector"](dve, link)

                def mask(u):
                    if u >= 4:
                        dve.wait_ge(sloped, u - 3)
                        dve.wait_ge(shifted, u - 3)
                    if scores:
                        dve.wait_ge(scored, u + 1)
                    nc.vector.tensor_tensor_reduce(
                        out=g[u % 4][:, :], in0=rows(u), in1=neg[:, u // heads, :], scale=1.0, scalar=-3e38,
                        op0=ALU.add, op1=ALU.max, accum_out=gm[:, u:u + 1]).then_inc(maxed, 1)

                def shift(u):
                    dve.wait_ge(sloped, u + 1)
                    if u >= 2:
                        dve.wait_ge(turned, 2 * (u - 1))
                    nc.vector.scalar_tensor_tensor(
                        out=lm[u % 2][:, :], in0=g[u % 4][:, :], scalar=b1[:, u:u + 1], in1=t2[u % 4][:, :],
                        op0=ALU.add, op1=ALU.min if lowest(u) else ALU.max).then_inc(shifted, 1)

                def end(u):
                    dve.wait_ge(weighed, u + 1)
                    finish(u, dve, link, o[u % 2]).then_inc(finished, 1)

                for u in range(units + 4):
                    if u < units:
                        mask(u)
                    if 2 <= u < units + 2:
                        shift(u - 2)
                    if u >= 4:
                        end(u - 4)
                if "vector_end" in extra:
                    link(nc.vector.memset(stats[:, 0, 0:1], 0.0))
                    extra["vector_end"](dve, link, gm)

            @block.gpsimd
            def _(pool):
                link = linker(pool, pool_done)
                if "pool" in extra:
                    extra["pool"](pool)
                for u in range(units):
                    c = slice(u, u + 1)
                    pool.wait_ge(maxed, u + 1)
                    link(nc.gpsimd.tensor_tensor(y[:, c], gm[:, c], s[:, c], ALU.add))
                    nc.gpsimd.tensor_scalar(ay[:, c], y[:, c], slope, None, ALU.mult)
                    link(nc.gpsimd.tensor_scalar(m[:, c], y[:, c], 0.0, 1.0 - slope,
                                                 ALU.min if lowest(u) else ALU.max, ALU.mult))
                    link(nc.gpsimd.tensor_tensor(m[:, c], m[:, c], ay[:, c], ALU.add))
                    nc.gpsimd.tensor_tensor(b1[:, c], s[:, c], m[:, c], ALU.subtract)
                    nc.gpsimd.tensor_tensor(b2[:, c], sa[:, c], m[:, c], ALU.subtract).then_inc(biased, 1)

            @block.scalar
            def _(act):
                if "scalar" in extra:
                    extra["scalar"](act)

                def slope_of(u):
                    act.wait_ge(biased, u + 1)
                    if u >= 4:
                        act.wait_ge(shifted, u - 3)
                    nc.scalar.activation(t2[u % 4][:, :], g[u % 4][:, :], ACT.Identity, bias=b2[:, u:u + 1],
                                         scale=slope).then_inc(sloped, 1)

                def exp_of(u):
                    for hf in range(2):
                        act.wait_ge(turned, 2 * u + hf + 1)
                        if u >= 2 and hf == 0:
                            act.wait_ge(weighed, u - 1)
                        q = slice(hf * NT // 2, (hf + 1) * NT // 2)
                        nc.scalar.activation(pT[u % 2][:, q, :], tp[u % 2][:, q, :], ACT.Exp)\
                            .then_inc(exped, 1)

                slope_of(0)
                for u in range(1, units + 3):
                    if u >= 3:
                        exp_of(u - 3)
                    if u < units:
                        slope_of(u)

            @block.tensor
            def _(pe):
                if "tensor" in extra:
                    extra["tensor"](pe)

                def turn(u):
                    pe.wait_ge(shifted, u + 1)
                    for hf in range(2):
                        if u >= 2:
                            pe.wait_ge(exped, 2 * (u - 2) + hf + 1)
                        for c in range(hf * NT // 2, (hf + 1) * NT // 2):
                            ins = nc.tensor.transpose(tp[u % 2][:, c, :], lm[u % 2][:, c * P:(c + 1) * P],
                                                      ident[:, :])
                        ins.then_inc(turned, 1)

                def weigh(u):
                    if u >= 2:
                        pe.wait_ge(finished, u - 1)
                    for c in range(NT):
                        if c % (NT // 2) == 0:
                            pe.wait_ge(exped, 2 * u + c // (NT // 2) + 1)
                        ins = nc.tensor.matmul(o[u % 2][:, 0:width], pT[u % 2][:, c, :], values(u, c),
                                               start=(c == 0), stop=(c == NT - 1))
                    ins.then_inc(weighed, 1)

                if scores:
                    scores(0).then_inc(scored, 1)
                for u in range(units + 3):
                    if 2 <= u < units + 2:
                        turn(u - 2)
                    if scores and u + 1 < units:
                        pe.wait_ge(maxed, u + 1)
                        scores(u + 1).then_inc(scored, 1)
                    if u >= 3:
                        weigh(u - 3)
                if "tensor_end" in extra:
                    extra["tensor_end"](pe)

        def graph0():
            HID, OUT, ED = 32, 128, 32
            with Phase("g0") as ph:
                s = ph.sb("s", [P, NT])
                sa = ph.sb("sa", [P, NT])
                xa = ph.sb("xa", [HID, N])
                na = ph.sb("na", [HID, N])
                V = ph.sb("V", [P, NT, OUT + 1])
                f01 = ph.sb("f01", [P, 2, OUT])
                with Phase("p0") as pp:
                    neighT = pp.sb("neighT", [P, DC, N])
                    adj = pp.sb("adj", [P, NT, N], I32)
                    neigh_loaded = pp.sem("neigh_loaded")
                    adj_loaded = [pp.sem(f"adj_loaded{t}") for t in range(NT)]
                    with Phase("init") as pi:
                        constants(pi, neighT, neigh_loaded)
                    wx1, wn1 = pp.sb("wx1", [P, DC, HID]), pp.sb("wn1", [P, DC, HID])
                    wx2, wn2, we = (pp.sb(n, [HID, HID]) for n in ("wx2", "wn2", "we"))
                    cols = pp.sb("cols", [HID, 5])
                    wv, wfx = pp.sb("wv", [P, DC, OUT]), pp.sb("wfx", [P, DC, OUT])
                    wfe = pp.sb("wfe", [ED, OUT])
                    emb = pp.sb("emb", [ED, 2])
                    rowsb = pp.sb("rowsb", [P, 3, OUT])
                    emb_b = pp.sb("emb_b", [ED, 2, P])
                    tx, tn = pp.sb("tx", [HID, N]), pp.sb("tn", [HID, N])
                    eatt = pp.sb("eatt", [HID, 2])
                    tps = [pp.ps(f"tps{n}", [P, DC, P]) for n in range(2)]
                    psA = pp.ps("psA", [P, 2, 512])
                    psB = pp.ps("psB", [P, 2, 512])
                    loaded = pp.sem("loaded")
                    var_ready, rstd_ready = pp.sem("var_ready"), pp.sem("rstd_ready")
                    xn_ready, tp_ready, xnT_ready = pp.sem("xn"), pp.sem("tp"), pp.sem("xnT")
                    vd, mm, copied, tanhed = pp.sem("vd"), pp.sem("mm"), pp.sem("copied"), pp.sem("tanhed")
                    blk = pp.block()
                    loads = [(w[:, :, :], A[n].rearrange("(c p) n -> p c n", p=P)) for w, n in
                              ((wx1, "L0_gnn_Wx1"), (wn1, "L0_gnn_Wn1"), (wv, "L0_gnn_Wv"), (wfx, "L0_gnn_Wfx"))]
                    loads += [(w[:, :], A[n]) for w, n in ((wx2, "L0_gnn_Wx2"), (wn2, "L0_gnn_Wn2"),
                                                           (we, "L0_gnn_We"), (wfe, "L0_gnn_Wfe"))]
                    loads += [(cols[:, n:n + 1], A[b].unsqueeze(1)) for n, b in
                              enumerate(("L0_gnn_bx1", "L0_gnn_bx2", "L0_gnn_bn1", "L0_gnn_bn2", "L0_gnn_be"))]
                    loads += [(rowsb[:, n, :], A[b].unsqueeze(0).to_broadcast([P, OUT])) for n, b in
                              enumerate(("L0_gnn_bv", "L0_gnn_bfx", "L0_gnn_bfe"))]
                    loads += [(emb[:, n:n + 1], A["L0_gnn_edge_emb"][n, :].unsqueeze(1)) for n in range(2)]
                    ALL = 16 * len(loads)

                    @blk.sync
                    def _(sp):
                        for dst, src in loads:
                            sp.dma_start(dst, src).then_inc(loaded, 16)
                        for t in range(NT):
                            sp.dma_start(adj[:, t, :], A["adj"][t * P:(t + 1) * P, :]).then_inc(adj_loaded[t], 16)
                        sp.wait_ge(loaded, ALL)
                        sp.wait_ge(neigh_loaded, 16)

                    @blk.tensor
                    def _(pe):
                        norm_tensor(pe, tps, xn_ready, tp_ready, xnT_ready)
                        pe.wait_ge(loaded, ALL)
                        pe.wait_ge(neigh_loaded, 16)
                        pe.wait_ge(xnT_ready, NT)
                        for w, src, ps in ((wx1, xnT, psA), (wn1, neighT, psB)):
                            for hf in range(2):
                                for c in range(DC):
                                    ins = nc.tensor.matmul(ps[0:HID, hf, :], w[:, c, :],
                                                           src[:, c, hf * 512:(hf + 1) * 512],
                                                           start=(c == 0), stop=(c == DC - 1))
                            ins.then_inc(mm, 1)
                        for n, (w, src, ps) in enumerate(((wx2, tx, psA), (wn2, tn, psB))):
                            pe.wait_ge(tanhed, n + 1)
                            for hf in range(2):
                                ins = nc.tensor.matmul(ps[0:HID, hf, :], w[:, :], src[:, hf * 512:(hf + 1) * 512],
                                                       start=True, stop=True)
                            ins.then_inc(mm, 1)
                        pe.wait_ge(copied, 2)
                        nc.tensor.matmul(psA[0:HID, 0, 0:2], we[:, :], emb[:, :], start=True, stop=True)\
                            .then_inc(mm, 1)
                        pe.wait_ge(tanhed, 3)
                        for t in range(NT):
                            ins = nc.tensor.matmul(psA[:, 1, t:t + 1], xa[:, t * P:(t + 1) * P], eatt[:, 1:2],
                                                   start=True, stop=True)
                        ins.then_inc(mm, 1)
                        for n in range(2):
                            ins = nc.tensor.matmul(psB[:, 0, n * OUT:(n + 1) * OUT], emb_b[:, n, :], wfe[:, :],
                                                   start=True, stop=True)
                        ins.then_inc(mm, 1)
                        pe.wait_ge(copied, 4)
                        for t in range(NT):
                            if t >= 2:
                                pe.wait_ge(copied, 4 + t - 1)
                            ps = (psA, psB)[t % 2]
                            for n, (src, w) in enumerate(((neighT, wv), (xnT, wfx))):
                                for c in range(DC):
                                    ins = nc.tensor.matmul(ps[:, n, 0:OUT], src[:, c, t * P:(t + 1) * P], w[:, c, :],
                                                           start=(c == 0), stop=(c == DC - 1))
                            ins.then_inc(mm, 1)

                    @blk.gpsimd
                    def _(pool):
                        norm_gpsimd(pool, var_ready, rstd_ready)

                    @blk.scalar
                    def _(act):
                        norm_scalar(act, tps, tp_ready, xnT_ready)
                        act.wait_ge(loaded, ALL)
                        for n, (t, ps) in enumerate(((tx, psA), (tn, psB))):
                            act.wait_ge(mm, n + 1)
                            nc.scalar.activation(t[:, :].rearrange("p (a b) -> p a b", a=2), ps[0:HID, :, :],
                                                 ACT.Tanh, bias=cols[:, 2 * n:2 * n + 1]).then_inc(tanhed, 1)
                        act.wait_ge(mm, 5)
                        nc.scalar.activation(eatt[:, :], psA[0:HID, 0, 0:2], ACT.Tanh, bias=cols[:, 4:5])\
                            .then_inc(tanhed, 1)

                    @blk.vector
                    def _(dve):
                        link = linker(dve, vd)
                        norm_vector(dve, link, var_ready, rstd_ready, xn_ready)
                        nc.vector.memset(V[:, :, OUT:OUT + 1], 1.0)
                        dve.wait_ge(loaded, ALL)

                        def mask_of(t):
                            dve.wait_ge(adj_loaded[t], 16)
                            nc.vector.tensor_scalar(neg[:, t, :], adj[:, t, :], 0.0, MASKED, ALU.is_le, ALU.mult)

                        nc.vector.tensor_copy(emb_b[:, 0, :], bc(emb[:, 0:1], [ED, P]))
                        link(nc.vector.tensor_copy(emb_b[:, 1, :], bc(emb[:, 1:2], [ED, P])))
                        for t in range(4):
                            mask_of(t)
                        for n, (t, ps) in enumerate(((xa, psA), (na, psB))):
                            dve.wait_ge(mm, 3 + n)
                            nc.vector.tensor_scalar(t[:, :].rearrange("p (a b) -> p a b", a=2), ps[0:HID, :, :],
                                                    cols[:, 2 * n + 1:2 * n + 2], None, ALU.add).then_inc(copied, 1)
                        dve.wait_ge(mm, 6)
                        nc.vector.tensor_copy(s[:, :], psA[:, 1, 0:NT])
                        nc.vector.tensor_scalar(sa[:, :], psA[:, 1, 0:NT], 0.01, None, ALU.mult).then_inc(copied, 1)
                        dve.wait_ge(mm, 7)
                        nc.vector.tensor_tensor(f01[:, :, :], psB[:, 0, 0:2 * OUT].rearrange("p (a b) -> p a b", a=2),
                                                bc(rowsb[:, 2:3, :], [P, 2, OUT]), ALU.add).then_inc(copied, 1)
                        for t in range(4, NT):
                            mask_of(t)
                        for t in range(NT):
                            dve.wait_ge(mm, 8 + t)
                            ps = (psA, psB)[t % 2]
                            nc.vector.tensor_tensor(V[:, t, 0:OUT], ps[:, 0, 0:OUT], rowsb[:, 0, :], ALU.add)
                            link(nc.vector.tensor_tensor(x[:, t, 0:OUT], ps[:, 1, 0:OUT], x[:, t, 0:OUT], ALU.add))
                            nc.vector.tensor_tensor(x[:, t, 0:OUT], x[:, t, 0:OUT], rowsb[:, 1, :], ALU.add)\
                                .then_inc(copied, 1)

                S = ph.ps("S", [P, 2, 512])
                r = ph.sb("r", [P, NT])
                has = ph.sb("has", [P, NT])
                block = ph.block()

                def scores(u):
                    for hf in range(2):
                        ins = nc.tensor.matmul(S[:, hf, :], xa[:, u * P:(u + 1) * P],
                                               na[:, hf * 512:(hf + 1) * 512], start=True, stop=True)
                    return ins

                def finish(u, dve, link, o):
                    link(nc.vector.reciprocal(r[:, u:u + 1], o[:, OUT:OUT + 1]))
                    return nc.vector.scalar_tensor_tensor(
                        out=x[:, u, OUT:D], in0=o[:, 0:OUT], scalar=r[:, u:u + 1], in1=x[:, u, OUT:D],
                        op0=ALU.mult, op1=ALU.add)

                def vector_end(dve, link, gm):
                    nc.vector.tensor_scalar(has[:, :], gm, MASKED / 2, None, ALU.is_gt)
                    link(nc.vector.tensor_tensor(f01[:, 1, :], f01[:, 1, :], f01[:, 0, :], ALU.subtract))
                    link(nc.vector.tensor_tensor(x[:, :, OUT:D], x[:, :, OUT:D],
                                                 bc(f01[:, 0:1, :], [P, NT, OUT]), ALU.add))
                    for t in range(NT):
                        nc.vector.scalar_tensor_tensor(
                            out=x[:, t, OUT:D], in0=f01[:, 1, :], scalar=has[:, t:t + 1], in1=x[:, t, OUT:D],
                            op0=ALU.mult, op1=ALU.add)

                attention(block, ph, 1, 0.01, lambda u: False, lambda u: S[:, :, :].rearrange("p a b -> p (a b)"),
                          s, sa, lambda u, c: V[:, c, :], OUT + 1, finish, scores, {"vector_end": vector_end})

        def graph1():
            H, DH, SLOPE = 4, 64, 0.2
            with Phase("g1") as ph:
                s = ph.sb("s", [P, NT, H])
                sa = ph.sb("sa", [P, NT, H])
                dst = ph.sb("dst", [P, H, N])
                V = ph.sb("V", [P, NT, H, DH + 1])
                with Phase("p1") as pp:
                    hT = pp.sb("hT", [P, DC, N])
                    w = pp.sb("w", [P, DC, D])
                    a_src = pp.sb("a_src", [P, DC, H])
                    a_dst = pp.sb("a_dst", [P, H, 1])
                    a_dstb = pp.sb("a_dstb", [P, H, P])
                    tps = [pp.ps(f"tps{n}", [P, DC, P]) for n in range(2)]
                    ps = [pp.ps(f"ps{n}", [P, 512]) for n in range(4)]
                    loaded, zeroed = pp.sem("loaded"), pp.sem("zeroed")
                    var_ready, rstd_ready = pp.sem("var_ready"), pp.sem("rstd_ready")
                    xn_ready, tp_ready, xnT_ready = pp.sem("xn"), pp.sem("tp"), pp.sem("xnT")
                    vd, mm, copied, spread = pp.sem("vd"), pp.sem("mm"), pp.sem("copied"), pp.sem("spread")
                    blk = pp.block()
                    ALL = 16 * (1 + 2 * H)

                    @blk.sync
                    def _(sp):
                        sp.dma_start(w[:, :, :], A["L1_gnn_WT"].rearrange("(c p) n -> p c n", p=P)).then_inc(loaded, 16)
                        sp.wait_ge(zeroed, 1)
                        for h in range(H):
                            part = slice(h % 2 * DH, (h % 2 + 1) * DH)
                            sp.dma_start(a_src[part, h // 2, h:h + 1], A["L1_gnn_a_src"][h, :].unsqueeze(1))\
                                .then_inc(loaded, 16)
                            sp.dma_start(a_dst[part, h, :], A["L1_gnn_a_dst"][h, :].unsqueeze(1)).then_inc(loaded, 16)
                        sp.wait_ge(loaded, ALL)

                    @blk.tensor
                    def _(pe):
                        norm_tensor(pe, tps, xn_ready, tp_ready, xnT_ready)
                        pe.wait_ge(loaded, ALL)
                        pe.wait_ge(xnT_ready, NT)
                        n = 0
                        for fc in range(DC):
                            for hf in range(2):
                                for c in range(DC):
                                    ins = nc.tensor.matmul(ps[n % 4][:, :], w[:, c, fc * P:(fc + 1) * P],
                                                           xnT[:, c, hf * 512:(hf + 1) * 512],
                                                           start=(c == 0), stop=(c == DC - 1))
                                ins.then_inc(mm, 1)
                                n += 1
                        for t in range(NT):
                            pe.wait_ge(copied, n - 3)
                            for c in range(DC):
                                ins = nc.tensor.matmul(ps[n % 4][:, 0:D], xnT[:, c, t * P:(t + 1) * P], w[:, c, :],
                                                       start=(c == 0), stop=(c == DC - 1))
                            ins.then_inc(mm, 1)
                            n += 1
                        pe.wait_ge(spread, 1)
                        for h in range(H):
                            for hf in range(2):
                                pe.wait_ge(copied, n - 3)
                                nc.tensor.matmul(ps[n % 4][:, :], a_dstb[:, h, :], hT[:, h // 2, hf * 512:(hf + 1) * 512],
                                                 start=True, stop=True).then_inc(mm, 1)
                                n += 1
                        pe.wait_ge(copied, n - 3)
                        for t in range(NT):
                            for fc in range(DC):
                                ins = nc.tensor.matmul(ps[n % 4][:, t * H:(t + 1) * H], hT[:, fc, t * P:(t + 1) * P],
                                                       a_src[:, fc, :], start=(fc == 0), stop=(fc == DC - 1))
                        ins.then_inc(mm, 1)

                    @blk.gpsimd
                    def _(pool):
                        norm_gpsimd(pool, var_ready, rstd_ready)

                    @blk.scalar
                    def _(act):
                        norm_scalar(act, tps, tp_ready, xnT_ready)

                    @blk.vector
                    def _(dve):
                        link = linker(dve, vd)
                        nc.vector.memset(a_src[:, :, :], 0.0)
                        nc.vector.memset(a_dst[:, :, :], 0.0).then_inc(zeroed, 1)
                        norm_vector(dve, link, var_ready, rstd_ready, xn_ready)
                        nc.vector.memset(V[:, :, :, DH:DH + 1], 1.0)
                        dve.wait_ge(loaded, ALL)
                        nc.vector.tensor_copy(a_dstb[:, :, :], bc(a_dst[:, :, :], [P, H, P])).then_inc(spread, 1)
                        n = 0
                        for fc in range(DC):
                            for hf in range(2):
                                dve.wait_ge(mm, n + 1)
                                nc.vector.tensor_copy(hT[:, fc, hf * 512:(hf + 1) * 512], ps[n % 4][:, :])\
                                    .then_inc(copied, 1)
                                n += 1
                        for t in range(NT):
                            dve.wait_ge(mm, n + 1)
                            nc.vector.tensor_copy(V[:, t, :, 0:DH],
                                                  ps[n % 4][:, 0:D].rearrange("p (h d) -> p h d", h=H)).then_inc(copied, 1)
                            n += 1
                        for h in range(H):
                            for hf in range(2):
                                dve.wait_ge(mm, n + 1)
                                nc.vector.tensor_copy(dst[:, h, hf * 512:(hf + 1) * 512], ps[n % 4][:, :])\
                                    .then_inc(copied, 1)
                                n += 1
                        dve.wait_ge(mm, n + 1)
                        src = ps[n % 4][:, 0:NT * H].rearrange("p (t h) -> p t h", h=H)
                        nc.vector.tensor_copy(s[:, :, :], src)
                        nc.vector.tensor_scalar(sa[:, :, :], src, SLOPE, None, ALU.mult).then_inc(copied, 1)

                r = ph.sb("r", [P, NT * H])
                block = ph.block()

                def finish(u, dve, link, o):
                    t, h = divmod(u, H)
                    link(nc.vector.reciprocal(r[:, u:u + 1], o[:, DH:DH + 1]))
                    return nc.vector.scalar_tensor_tensor(
                        out=x[:, t, h * DH:(h + 1) * DH], in0=o[:, 0:DH], scalar=r[:, u:u + 1],
                        in1=x[:, t, h * DH:(h + 1) * DH], op0=ALU.mult, op1=ALU.add)

                attention(block, ph, H, SLOPE, lambda u: False, lambda u: dst[:, u % H, :],
                          s[:, :, :].rearrange("p t h -> p (t h)"), sa[:, :, :].rearrange("p t h -> p (t h)"),
                          lambda u, c: V[:, c, u % H, :], DH + 1, finish, None, {})

        def graph2():
            KINDS = 3
            with Phase("g2") as ph:
                w = ph.sb("w", [P, DC, KINDS, D])
                high, low = (ph.sb(n, [P, NT, KINDS, D], F32R) for n in ("high", "low"))
                first12 = [ph.sb(f"first12{n}", [P, KINDS, D]) for n in range(2)]
                cut, rounded = ph.sem("cut"), ph.sem("rounded")
                bias = ph.sb("bias", [P, D])
                adjT = [ph.sb(f"adjT{n}", [P, NT, P], I32) for n in range(2)]
                mask = [ph.sb(f"mask{n}", [P, KINDS, NT, P], F32R) for n in range(2)]
                tps = [ph.ps(f"tps{n}", [P, DC, P]) for n in range(2)]
                psh = [ph.ps(f"psh{n}", [P, KINDS + 1, D]) for n in range(2)]
                pso = [ph.ps(f"pso{n}", [P, D]) for n in range(2)]
                loaded, vd, mm, split = ph.sem("loaded"), ph.sem("vd"), ph.sem("mm"), ph.sem("split")
                adjT_loaded = [ph.sem(f"adjT_loaded{n}") for n in range(2)]
                masked, summed, added = ph.sem("masked"), ph.sem("summed"), ph.sem("added")
                var_ready, rstd_ready = ph.sem("var_ready"), ph.sem("rstd_ready")
                xn_ready, tp_ready, xnT_ready = ph.sem("xn"), ph.sem("tp"), ph.sem("xnT")
                block = ph.block()
                adjT_v = A["adjT"].rearrange("(c p) i -> p c i", p=P)

                @block.sync
                def _(sp):
                    for v in range(KINDS):
                        sp.dma_start(w[:, :, v, :], A[f"L2_gnn_w{v + 1}"].rearrange("(c p) n -> p c n", p=P))\
                            .then_inc(loaded, 16)
                    sp.dma_start(bias[:, :], A["L2_gnn_bias"].unsqueeze(0).to_broadcast([P, D])).then_inc(loaded, 16)
                    for t in range(NT):
                        if t >= 2:
                            sp.wait_ge(masked, t - 1)
                        sp.dma_start(adjT[t % 2][:, :, :], adjT_v[:, :, t * P:(t + 1) * P])\
                            .then_inc(adjT_loaded[t % 2], 16)
                    sp.wait_ge(masked, NT)

                @block.tensor
                def _(pe):
                    norm_tensor(pe, tps, xn_ready, tp_ready, xnT_ready)
                    pe.wait_ge(loaded, 16 * (KINDS + 1))
                    for t in range(NT):
                        pe.wait_ge(xnT_ready, t + 1)
                        if t >= 2:
                            pe.wait_ge(split, t - 1)
                        for v in range(KINDS):
                            for c in range(DC):
                                ins = nc.tensor.matmul(psh[t % 2][:, v, :], xnT[:, c, t * P:(t + 1) * P],
                                                       w[:, c, v, :], start=(c == 0), stop=(c == DC - 1))
                        ins.then_inc(mm, 1)
                    pe.wait_ge(split, NT)
                    pe.wait_ge(rounded, NT)
                    for t in range(NT):
                        pe.wait_ge(masked, t + 1)
                        if t >= 2:
                            pe.wait_ge(added, t - 1)
                        for v in range(KINDS):
                            for c in range(NT):
                                for part in (high, low):
                                    ins = nc.tensor.matmul(
                                        pso[t % 2][:, :], mask[t % 2][:, v, c, :], part[:, c, v, :],
                                        start=(v == 0 and c == 0 and part is high),
                                        stop=(v == KINDS - 1 and c == NT - 1 and part is low))
                        ins.then_inc(summed, 1)

                @block.gpsimd
                def _(pool):
                    norm_gpsimd(pool, var_ready, rstd_ready)

                @block.scalar
                def _(act):
                    norm_scalar(act, tps, tp_ready, xnT_ready)
                    for t in range(NT):
                        act.wait_ge(cut, t + 1)
                        nc.scalar.activation(high[:, t, :, :], first12[t % 2][:, :, :], ACT.Copy).then_inc(rounded, 1)

                @block.vector
                def _(dve):
                    link = linker(dve, vd)
                    norm_vector(dve, link, var_ready, rstd_ready, xn_ready)
                    dve.wait_ge(loaded, 16 * (KINDS + 1))
                    dve.wait_ge(xn_ready, NT)
                    link(nc.vector.tensor_tensor(x[:, :, :], x[:, :, :], bc(bias[:, :].unsqueeze(1), [P, NT, D]), ALU.add))

                    def take(t):
                        dve.wait_ge(mm, t + 1)
                        if t >= 2:
                            dve.wait_ge(rounded, t - 1)
                        nc.vector.tensor_scalar(first12[t % 2][:, :, :].bitcast(I32),
                                                psh[t % 2][:, 0:KINDS, :].bitcast(I32),
                                                -(1 << 12), None, ALU.bitwise_and).then_inc(cut, 1)
                        dve.wait_ge(cut, t + 1)
                        nc.vector.tensor_tensor(low[:, t, :, :], psh[t % 2][:, 0:KINDS, :], first12[t % 2][:, :, :],
                                                ALU.subtract).then_inc(split, 1)

                    def masks(t):
                        dve.wait_ge(adjT_loaded[t % 2], 16 * (t // 2 + 1))
                        if t >= 2:
                            dve.wait_ge(summed, t - 1)
                        for v in range(KINDS):
                            ins = nc.vector.tensor_scalar(mask[t % 2][:, v, :, :], adjT[t % 2][:, :, :], float(v + 1),
                                                          None, ALU.is_equal)
                        ins.then_inc(masked, 1)

                    masks(0)
                    for t in range(NT):
                        take(t)
                    for t in range(NT):
                        if t + 1 < NT:
                            masks(t + 1)
                        dve.wait_ge(summed, t + 1)
                        nc.vector.tensor_tensor(x[:, t, :], x[:, t, :], pso[t % 2][:, :], ALU.add).then_inc(added, 1)

        def graph3():
            SLOPE = 0.2
            with Phase("g3") as ph:
                s = ph.sb("s", [P, NT, 2])
                sa = ph.sb("sa", [P, NT, 2])
                dst = ph.sb("dst", [P, 2, N])
                hp = ph.sb("hp", [P, NT, 2, D])
                with Phase("p3") as pp:
                    hT = pp.sb("hT", [P, DC, N])
                    w = pp.sb("w", [P, DC, D])
                    a = pp.sb("a", [P, 2, DC, 1])
                    a2b = pp.sb("a2b", [P, DC, P])
                    tps = [pp.ps(f"tps{n}", [P, DC, P]) for n in range(2)]
                    ps = [pp.ps(f"ps{n}", [P, 512]) for n in range(4)]
                    loaded = pp.sem("loaded")
                    var_ready, rstd_ready = pp.sem("var_ready"), pp.sem("rstd_ready")
                    xn_ready, tp_ready, xnT_ready = pp.sem("xn"), pp.sem("tp"), pp.sem("xnT")
                    vd, mm, copied, spread = pp.sem("vd"), pp.sem("mm"), pp.sem("copied"), pp.sem("spread")
                    blk = pp.block()

                    @blk.sync
                    def _(sp):
                        sp.dma_start(w[:, :, :], A["L3_gnn_W"].rearrange("(c p) n -> p c n", p=P)).then_inc(loaded, 16)
                        sp.dma_start(a[:, :, :, :].rearrange("p k c o -> p (k c o)"),
                                     A["L3_gnn_aT"]).then_inc(loaded, 16)
                        sp.wait_ge(loaded, 32)

                    @blk.tensor
                    def _(pe):
                        norm_tensor(pe, tps, xn_ready, tp_ready, xnT_ready)
                        pe.wait_ge(loaded, 32)
                        pe.wait_ge(xnT_ready, NT)
                        n = 0
                        for fc in range(DC):
                            for hf in range(2):
                                for c in range(DC):
                                    ins = nc.tensor.matmul(ps[n][:, :], w[:, c, fc * P:(fc + 1) * P],
                                                           xnT[:, c, hf * 512:(hf + 1) * 512],
                                                           start=(c == 0), stop=(c == DC - 1))
                                ins.then_inc(mm, 1)
                                n += 1
                        pe.wait_ge(spread, 1)
                        pe.wait_ge(copied, 4)
                        for hf in range(2):
                            for fc in range(DC):
                                ins = nc.tensor.matmul(ps[hf][:, :], a2b[:, fc, :], hT[:, fc, hf * 512:(hf + 1) * 512],
                                                       start=(fc == 0), stop=(fc == DC - 1))
                            ins.then_inc(mm, 1)
                        for t in range(NT):
                            for fc in range(DC):
                                ins = nc.tensor.matmul(ps[2][:, t:t + 1], hT[:, fc, t * P:(t + 1) * P], a[:, 0, fc, :],
                                                       start=(fc == 0), stop=(fc == DC - 1))
                        ins.then_inc(mm, 1)

                    @blk.gpsimd
                    def _(pool):
                        norm_gpsimd(pool, var_ready, rstd_ready)

                    @blk.scalar
                    def _(act):
                        norm_scalar(act, tps, tp_ready, xnT_ready)

                    @blk.vector
                    def _(dve):
                        link = linker(dve, vd)
                        norm_vector(dve, link, var_ready, rstd_ready, xn_ready)
                        dve.wait_ge(loaded, 32)
                        nc.vector.tensor_copy(a2b[:, :, :], bc(a[:, 1, :, :], [P, DC, P])).then_inc(spread, 1)
                        n = 0
                        for fc in range(DC):
                            for hf in range(2):
                                dve.wait_ge(mm, n + 1)
                                nc.vector.tensor_copy(hT[:, fc, hf * 512:(hf + 1) * 512], ps[n][:, :]).then_inc(copied, 1)
                                n += 1
                        for hf in range(2):
                            dve.wait_ge(mm, 5 + hf)
                            nc.vector.tensor_copy(dst[:, 0, hf * 512:(hf + 1) * 512], ps[hf][:, :])
                            nc.vector.tensor_scalar(dst[:, 1, hf * 512:(hf + 1) * 512], ps[hf][:, :], -1.0, None, ALU.mult)
                        dve.wait_ge(mm, 7)
                        for q, (o, f) in enumerate(((s, 1.0), (sa, SLOPE))):
                            for sign in range(2):
                                nc.vector.tensor_scalar(o[:, :, sign], ps[2][:, 0:NT], -f if sign else f, None, ALU.mult)

                r = ph.sb("r", [P, NT * 2])
                with Phase("a3") as pa:
                    block = pa.block()

                    def finish(u, dve, link, o):
                        t, sign = divmod(u, 2)
                        link(nc.vector.reciprocal(r[:, u:u + 1], o[:, D:D + 1]))
                        return nc.vector.tensor_scalar(hp[:, t, sign, :], o[:, 0:D], r[:, u:u + 1],
                                                       -1.0 if sign else 1.0, ALU.mult, ALU.mult)

                    attention(block, pa, 2, SLOPE, lambda u: u % 2 == 1, lambda u: dst[:, u % 2, :],
                              s[:, :, :].rearrange("p t h -> p (t h)"), sa[:, :, :].rearrange("p t h -> p (t h)"),
                              lambda u, c: xn[:, c, :], D + 1, finish, None, {})
                K4 = 2 * D // P
                wt = ph.sb("wt", [P, K4, D])
                hpT = ph.sb("hpT", [P, 2, K4, P])
                low, ex, z = ph.sb("low", [P, 2, D]), ph.sb("ex", [P, 2, D]), ph.sb("z", [P, 2, D])
                tp = [ph.ps(f"tp{n}", [P, K4, P]) for n in range(2)]
                pz = [ph.ps(f"pz{n}", [P, D]) for n in range(2)]
                loaded, turned, hpT_ready, mm = ph.sem("loaded"), ph.sem("turned"), ph.sem("hpT_ready"), ph.sem("mm")
                low_ready, ex_ready, done, vd = ph.sem("low_ready"), ph.sem("ex_ready"), ph.sem("done"), ph.sem("vd")
                block = ph.block()

                @block.sync
                def _(sp):
                    sp.dma_start(wt[:, :, :], A["L3_gnn_wtrans"].rearrange("(k p) n -> p k n", p=P)).then_inc(loaded, 16)
                    sp.wait_ge(loaded, 16)

                @block.tensor
                def _(pe):
                    def turn(t):
                        if t >= 2:
                            pe.wait_ge(hpT_ready, t - 1)
                        for k in range(K4):
                            ins = nc.tensor.transpose(tp[t % 2][:, k, :], hp[:, t, k // DC, k % DC * P:(k % DC + 1) * P],
                                                      ident[:, :])
                        ins.then_inc(turned, 1)
                    turn(0)
                    pe.wait_ge(loaded, 16)
                    for t in range(NT):
                        if t + 1 < NT:
                            turn(t + 1)
                        pe.wait_ge(hpT_ready, t + 1)
                        if t >= 2:
                            pe.wait_ge(done, t - 1)
                        for k in range(K4):
                            ins = nc.tensor.matmul(pz[t % 2][:, :], hpT[:, t % 2, k, :], wt[:, k, :],
                                                   start=(k == 0), stop=(k == K4 - 1))
                        ins.then_inc(mm, 1)

                @block.scalar
                def _(act):
                    for t in range(NT + 1):
                        if t < NT:
                            act.wait_ge(turned, t + 1)
                            if t >= 2:
                                act.wait_ge(mm, t - 1)
                            nc.scalar.activation(hpT[:, t % 2, :, :], tp[t % 2][:, :, :], ACT.Copy).then_inc(hpT_ready, 1)
                        if t >= 1:
                            act.wait_ge(low_ready, t)
                            nc.scalar.activation(ex[:, (t - 1) % 2, :], low[:, (t - 1) % 2, :], ACT.Exp)\
                                .then_inc(ex_ready, 1)

                @block.vector
                def _(dve):
                    link = linker(dve, vd)
                    for t in range(NT):
                        dve.wait_ge(mm, t + 1)
                        nc.vector.tensor_scalar(low[:, t % 2, :], pz[t % 2][:, :], 0.0, None, ALU.min).then_inc(low_ready, 1)
                        dve.wait_ge(ex_ready, t + 1)
                        link(nc.vector.scalar_tensor_tensor(out=z[:, t % 2, :], in0=pz[t % 2][:, :], scalar=0.0,
                                                            in1=ex[:, t % 2, :], op0=ALU.max, op1=ALU.add))
                        nc.vector.scalar_tensor_tensor(out=x[:, t, :], in0=z[:, t % 2, :], scalar=-1.0, in1=x[:, t, :],
                                                       op0=ALU.add, op1=ALU.add).then_inc(done, 1)

        def gate(L, E, gw_name, gb_name, all_probs, shared):
            first = NT if shared else 0
            T = loop_tiles(E, first)
            R = T - first
            with Phase(f"r{L}") as ph:
                gw = ph.sb("gw", [P, DC, E])
                gb = ph.sb("gb", [P, E])
                lg = ph.sb("lg", [P, NT, E])
                ez = ph.sb("ez", [P, NT, E])
                v8 = ph.sb("v8", [P, NT, 8])
                i8 = ph.sb("i8", [P, NT, 8], U32)
                idx = ph.sb("idx", [P, NT, 2])
                oh = ph.sb("oh", [P, 2, NT, E])
                both = ph.sb("both", [P, NT, E], BF16)
                cnt = ph.sb("cnt", [P, E, 1])
                over = ph.sb("over", [P, E, NT])
                tiles = ph.sb("tiles", [P, E])
                prev = ph.sb("prev", [P, E, E])
                base = ph.sb("base", [P, E])
                upto = ph.sb("upto", [P, E])
                rank = ph.sb("rank", [P, NT, E])
                prod = ph.sb("prod", [P, 2, NT, E])
                posf = ph.sb("posf", [P, 2, NT])
                pos = ph.sb("pos", [P, 2, NT], U32)
                row_f, none = ph.sb("row_f", [P, R]), ph.sb("none", [P, R])
                row_i = ph.sb("row_i", [P, R], U32)
                slot_i, tile_i = ph.sb("slot_i", [P, 2 * NT], U32), ph.sb("tile_i", [P, 2 * NT], U32)
                slot_f, tile_f = ph.sb("slot_f", [P, 2 * NT, 1]), ph.sb("tile_f", [P, 2 * NT, 1])
                on_slot = ph.sb("on_slot", [P, 2 * NT, P], BF16)
                on_tile = ph.sb("on_tile", [P, 2 * NT, R])
                token = ph.sb("token", [P, 2 * NT, 2, R], BF16)
                tokens = ph.sb("tokens", [P, 2, R])
                past = ph.sb("past", [1, R, E])
                et = ph.sb("et", [1, R])
                used = ph.sb("used", [1, NT])
                usedf = ph.sb("usedf", [1, 1])
                den = ph.sb("den", [P, 3, NT])
                tps = [ph.ps(f"tps{n}", [P, DC, P]) for n in range(4)]
                psl = ph.ps("psl", [P, NT, E])
                psr = ph.ps("psr", [P, NT, E])
                psc = ph.ps("psc", [P, E])
                pst = ph.ps("pst", [P, 2, R])
                loaded, vd, mm, exped = ph.sem("loaded"), ph.sem("vd"), ph.sem("mm"), ph.sem("exped")
                onehot, placed, centred = ph.sem("onehot"), ph.sem("placed"), ph.sem("centred")
                stored = ph.sem("stored")
                var_ready, rstd_ready = ph.sem("var_ready"), ph.sem("rstd_ready")
                xn_ready, tp_ready, xnT_ready = ph.sem("xn"), ph.sem("tp"), ph.sem("xnT")
                block = ph.block()
                ALL = 32 if gb_name else 16

                @block.sync
                def _(sp):
                    sp.dma_start(gw[:, :, :], A[gw_name].rearrange("(c p) n -> p c n", p=P)).then_inc(loaded, 16)
                    if gb_name:
                        sp.dma_start(gb[:, :], A[gb_name].unsqueeze(0).to_broadcast([P, E])).then_inc(loaded, 16)
                    sp.wait_ge(xn_ready, NT)
                    sp.dma_start(xn_rows.rearrange("(t p) d -> p t d", p=P), xn[:, :, 0:D]).then_inc(stored, 16)
                    sp.wait_ge(stored, 16)

                @block.tensor
                def _(pe):
                    def turn(t):
                        pe.wait_ge(xn_ready, t + 1)
                        if t >= 4:
                            pe.wait_ge(xnT_ready, t - 3)
                        for c in range(DC):
                            ins = nc.tensor.transpose(tps[t % 4][:, c, :], xn[:, t, c * P:(c + 1) * P], ident[:, :])
                        ins.then_inc(tp_ready, 1)

                    for t in range(3):
                        turn(t)
                    pe.wait_ge(loaded, ALL)
                    for t in range(NT):
                        if t + 3 < NT:
                            turn(t + 3)
                        pe.wait_ge(xnT_ready, t + 1)
                        for c in range(DC):
                            ins = nc.tensor.matmul(psl[:, t, :], xnT[:, c, t * P:(t + 1) * P], gw[:, c, :],
                                                   start=(c == 0), stop=(c == DC - 1))
                    ins.then_inc(mm, 1)
                    pe.wait_ge(onehot, 1)
                    for t in range(NT):
                        for q in range(t + 1):
                            nc.tensor.matmul(psr[:, t, :], (before_b if q == t else ones_b)[:, :], both[:, q, :],
                                             start=(q == 0), stop=(q == t))
                    for q in range(NT):
                        ins = nc.tensor.matmul(psc[:, :], ones_b[:, :], both[:, q, :], start=(q == 0), stop=(q == NT - 1))
                    ins.then_inc(mm, 1)
                    pe.wait_ge(placed, 1)
                    for q in range(2 * NT):
                        ins = nc.tensor.matmul(pst[:, :, :], on_slot[:, q, :], token[:, q, :, :],
                                               start=(q == 0), stop=(q == 2 * NT - 1))
                    ins.then_inc(mm, 1)

                @block.scalar
                def _(act):
                    norm_scalar(act, tps, tp_ready, xnT_ready)
                    act.wait_ge(centred, 1)
                    nc.scalar.activation(ez[:, :, :], ez[:, :, :], ACT.Exp)
                    nc.scalar.activation(den[:, 0, :], den[:, 0, :], ACT.Exp).then_inc(exped, 1)

                @block.gpsimd
                def _(pool):
                    norm_gpsimd(pool, var_ready, rstd_ready)

                @block.vector
                def _(dve):
                    link = linker(dve, vd)
                    norm_vector(dve, link, var_ready, rstd_ready, xn_ready)
                    dve.wait_ge(mm, 1)
                    dve.wait_ge(loaded, ALL)
                    if gb_name:
                        link(nc.vector.tensor_tensor(lg[:, :, :], psl[:, :, :], bc(gb[:, :].unsqueeze(1), [P, NT, E]),
                                                     ALU.add))
                    else:
                        link(nc.vector.tensor_copy(lg[:, :, :], psl[:, :, :]))
                    for t in range(NT):
                        ins = nc.vector.max(out=v8[:, t, :], in_=lg[:, t, :])
                    link(ins)
                    for t in range(NT):
                        ins = nc.vector.max_index(out=i8[:, t, :], in_max=v8[:, t, :], in_values=lg[:, t, :])
                    link(ins)
                    link(nc.vector.tensor_copy(idx[:, :, :], i8[:, :, 0:2]))
                    for k in range(2):
                        ins = nc.vector.tensor_tensor(oh[:, k, :, :], bc(iota_row[:, 0:E].unsqueeze(1), [P, NT, E]),
                                                      bc(idx[:, :, k:k + 1], [P, NT, E]), ALU.is_equal)
                    link(ins)
                    nc.vector.tensor_tensor(both[:, :, :], oh[:, 0, :, :], oh[:, 1, :, :], ALU.add).then_inc(onehot, 1)
                    nc.vector.tensor_tensor(ez[:, :, :], lg[:, :, :], bc(v8[:, :, 0:1], [P, NT, E]), ALU.subtract)
                    nc.vector.tensor_tensor(den[:, 0, :], v8[:, :, 1], v8[:, :, 0], ALU.subtract).then_inc(centred, 1)
                    dve.wait_ge(exped, 1)
                    if all_probs:
                        link(nc.vector.tensor_reduce(den[:, 1, :], ez[:, :, :], AX.X, ALU.add))
                    else:
                        link(nc.vector.tensor_scalar(den[:, 1, :], den[:, 0, :], 1.0, None, ALU.add))
                    link(nc.vector.reciprocal(wts[:, 0, :], den[:, 1, :]))
                    nc.vector.tensor_tensor(wts[:, 1, :], den[:, 0, :], wts[:, 0, :], ALU.mult)
                    dve.wait_ge(mm, 2)
                    link(nc.vector.tensor_copy(cnt[:, :, 0], psc[:, :]))
                    link(nc.vector.tensor_tensor(over[:, :, :], bc(cnt[:, :, :], [P, E, NT]),
                                                 bc(iota_128[:, :].unsqueeze(1), [P, E, NT]), ALU.is_gt))
                    link(nc.vector.tensor_reduce(tiles[:, :], over[:, :, :], AX.X, ALU.add))
                    link(nc.vector.tensor_tensor(prev[:, :, :], bc(tiles[:, :].unsqueeze(1), [P, E, E]),
                                                 before_e[:, 0:E, 0:E], ALU.mult))
                    link(nc.vector.tensor_reduce(base[:, :], prev[:, :, :], AX.X, ALU.add))
                    nc.vector.tensor_tensor(upto[:, :], base[:, :], tiles[:, :], ALU.add)
                    link(nc.vector.scalar_tensor_tensor(out=rank[:, :, :], in0=bc(base[:, :].unsqueeze(1), [P, NT, E]),
                                                        scalar=float(P), in1=psr[:, :, :], op0=ALU.mult, op1=ALU.add))
                    for k in range(2):
                        ins = nc.vector.tensor_tensor(prod[:, k, :, :], oh[:, k, :, :], rank[:, :, :], ALU.mult)
                    link(ins)
                    link(nc.vector.tensor_reduce(posf[:, :, :], prod[:, :, :, :], AX.X, ALU.add))
                    link(nc.vector.tensor_copy(pos[:, :, :], posf[:, :, :]))
                    pairs = pos[:, :, :].rearrange("p k t -> p (k t)")
                    nc.vector.tensor_scalar(slot_i[:, :], pairs, P - 1, None, ALU.bitwise_and)
                    link(nc.vector.tensor_scalar(tile_i[:, :], pairs, P.bit_length() - 1, None, ALU.logical_shift_right))
                    nc.vector.tensor_copy(slot_f[:, :, 0], slot_i[:, :])
                    link(nc.vector.tensor_copy(tile_f[:, :, 0], tile_i[:, :]))
                    link(nc.vector.tensor_tensor(on_tile[:, :, :], bc(iota_row[:, 0:R].unsqueeze(1), [P, 2 * NT, R]),
                                                 bc(tile_f[:, :, :], [P, 2 * NT, R]), ALU.is_equal))
                    nc.vector.tensor_tensor(token[:, :, 0, :], on_tile[:, :, :],
                                            bc(pair_row[:, :, :].rearrange("p k t -> p (k t)").unsqueeze(2), [P, 2 * NT, R]),
                                            ALU.mult)
                    nc.vector.tensor_scalar(token[:, :, 1, :], on_tile[:, :, :], iota_p[:, :], None, ALU.mult)
                    nc.vector.tensor_tensor(on_slot[:, :, :], bc(iota_row[:, :].unsqueeze(1), [P, 2 * NT, P]),
                                            bc(slot_f[:, :, :], [P, 2 * NT, P]), ALU.is_equal).then_inc(placed, 1)
                    link(nc.vector.tensor_tensor(past[:, :, :], bc(upto[0:1, :].unsqueeze(1), [1, R, E]),
                                                 bc(iota_row[0:1, 0:R].unsqueeze(2), [1, R, E]), ALU.is_le))
                    link(nc.vector.tensor_reduce(et[:, :], past[:, :, :], AX.X, ALU.add))
                    if shared:
                        nc.vector.memset(etab[0:1, 0:first], E)
                        nc.vector.tensor_copy(dest[:, 0:first], own[:, 0:first])
                    nc.vector.tensor_scalar(etab[0:1, first:T], et[:, :], float(E - 1), None, ALU.min)
                    link(nc.vector.tensor_scalar(used[:, :], iota_un[0:1, :], float(first), upto[0:1, E - 1:E],
                                                 ALU.subtract, ALU.is_lt))
                    link(nc.vector.tensor_reduce(usedf[:, :], used[:, :], AX.X, ALU.add))
                    nc.vector.tensor_scalar(more[:, :], usedf[:, :], -2.0, None, ALU.add)
                    dve.wait_ge(mm, 3)
                    link(nc.vector.tensor_copy(tokens[:, :, :], pst[:, :, :]))
                    link(nc.vector.scalar_tensor_tensor(out=row_f[:, :], in0=tokens[:, 0, :], scalar=float(P),
                                                        in1=tokens[:, 1, :], op0=ALU.mult, op1=ALU.add))
                    nc.vector.tensor_scalar(none[:, :], row_f[:, :], 0.0, None, ALU.is_equal)
                    link(nc.vector.tensor_scalar(row_f[:, :], row_f[:, :], -float(P), 0.0, ALU.add, ALU.max))
                    nc.vector.tensor_copy(row_i[:, :], row_f[:, :])
                    link(nc.vector.tensor_tensor(none[:, :], none[:, :], own[:, first:T], ALU.mult))
                    nc.vector.tensor_scalar(table[:, 0:R], row_i[:, :], N - 1, None, ALU.bitwise_and)
                    nc.vector.tensor_tensor(dest[:, first:T], none[:, :], row_f[:, :], ALU.add)

        def combine(ph, shared, post_norm, final, room):
            K = 3 if shared else 2
            yg = [room[t % UN][:, t // UN * K * D:(t // UN + 1) * K * D].rearrange("p (k d) -> p k d", d=D)
                  for t in range(NT)]
            y_loaded = [ph.sem(f"y_loaded{t}") for t in range(NT)]
            var_ready, rstd_ready = ph.sem("var_ready"), ph.sem("rstd_ready")
            loaded, vd, stored, ready = ph.sem("loaded"), ph.sem("vd"), ph.sem("stored"), ph.sem("ready")
            if post_norm:
                z = ph.sb("z", [P, NT, D])
                gamma, beta = ph.sb("gamma", [P, D]), ph.sb("beta", [P, D])

            def load(sp):
                y_v = y_rows[0:K * N, :].rearrange("(k t p) d -> p t k d", p=P, t=NT)
                for t in range(NT):
                    sp.dma_start(yg[t], y_v[:, t, :, :]).then_inc(y_loaded[t], 16)
                if post_norm:
                    for dst, name in ((gamma, "L0_ffn_gamma"), (beta, "L0_ffn_beta")):
                        sp.dma_start(dst[:, :], A[name].unsqueeze(0).to_broadcast([P, D])).then_inc(loaded, 16)
                    sp.wait_ge(loaded, 32)
                if final:
                    o_v = out.rearrange("(t p) d -> p t d", p=P)
                    for t in range(NT):
                        sp.wait_ge(ready, t + 1)
                        sp.dma_start(o_v[:, t, :], x[:, t, :]).then_inc(stored, 16)
                    sp.wait_ge(stored, 16 * NT)

            def rstds(pool):
                if post_norm:
                    norm_gpsimd(pool, var_ready, rstd_ready)

            def add(dve):
                link = linker(dve, vd)
                for t in range(NT):
                    acc = z[:, t, :] if post_norm else x[:, t, :]
                    dve.wait_ge(y_loaded[t], 16)
                    if shared:
                        link(nc.vector.tensor_tensor(acc, acc, yg[t][:, 2, :], ALU.add))
                    link(nc.vector.scalar_tensor_tensor(
                        out=acc, in0=yg[t][:, 0, :], scalar=wts[:, 0, t:t + 1],
                        in1=xn[:, t, 0:D] if post_norm else acc, op0=ALU.mult, op1=ALU.add))
                    nc.vector.scalar_tensor_tensor(out=acc, in0=yg[t][:, 1, :], scalar=wts[:, 1, t:t + 1],
                                                   in1=acc, op0=ALU.mult, op1=ALU.add).then_inc(ready, 1)
                if post_norm:
                    dve.wait_ge(ready, NT)
                    for t in range(NT):
                        ins = nc.vector.bn_stats(out=stats[:, t, :], in_=z[:, t, :])
                    link(ins)
                    for t in range(NT):
                        ins = nc.vector.bn_aggr(out=mean_var[:, t, :], in_=stats[:, t, :])
                    ins.then_inc(var_ready, 1)
                    dve.wait_ge(var_ready, 1)
                    dve.wait_ge(loaded, 32)
                    for t in range(NT):
                        ins = nc.vector.scalar_tensor_tensor(
                            out=z[:, t, :], in0=z[:, t, :], scalar=mean_var[:, t, 0:1], in1=gamma[:, :],
                            op0=ALU.subtract, op1=ALU.mult)
                    link(ins)
                    dve.wait_ge(rstd_ready, 2)
                    for t in range(NT):
                        ins = nc.vector.scalar_tensor_tensor(
                            out=z[:, t, :], in0=z[:, t, :], scalar=rstd[:, t, :], in1=beta[:, :],
                            op0=ALU.mult, op1=ALU.add)
                    link(ins)
                    nc.vector.tensor_tensor(x[:, :, :], x[:, :, :], z[:, :, :], ALU.add)
            return load, rstds, add

        def experts(L, E, F, kind, shared, w1_name, w2_name, b2_name, post_norm, final):
            first = NT if shared else 0
            T = loop_tiles(E, first)
            EN = E + shared
            FC = F // P
            up = 2 if kind == "silu" else 1
            W1C = up * DC * F + (0 if kind == "silu" else FC)
            LEAST = (first + 2 * N // P) // UN
            with Phase(f"e{L}") as ph:
                w1 = [ph.sb(f"w1{n}", [P, W1C]) for n in range(UN)]
                w2 = [ph.sb(f"w2{n}", [P, FC * D]) for n in range(UN)]
                b2 = [ph.sb(f"b2{n}", [P, D]) for n in range(UN)] if b2_name else None
                xs = [ph.sb(f"xs{n}", [P, D]) for n in range(UN)]
                ys = [ph.sb(f"ys{n}", [P, D]) for n in range(UN)]
                idx = [ph.sb(f"idx{n}", [P, 1], U32) for n in range(UN)]
                to = [ph.sb(f"to{n}", [P, 1], U32) for n in range(UN)]
                xsT = [ph.sb(f"xsT{n}", [P, DC, P]) for n in range(2)]
                hT = [xnT[:, n, 0:F].rearrange("p (f q) -> p f q", q=P) for n in range(2)]
                h_hi, h_lo = ([ph.sb(f"{k}{n}", [P, FC, P], F32R) for n in range(2)] for k in ("h_hi", "h_lo"))
                w2_hi, w2_lo = ([ph.sb(f"{k}{n}", [P, FC * D], F32R) for n in range(2)] for k in ("w2_hi", "w2_lo"))
                h_rounded, h_split = ph.sem("h_rounded"), ph.sem("h_split")
                w2_rounded, w2_split = ph.sem("w2_rounded"), ph.sem("w2_split")
                sg = [ph.sb(f"sg{n}", [P, FC, P]) for n in range(2)] if kind == "silu" else None
                pT = [ph.ps(f"pT{n}", [P, DC, P]) for n in range(2)]
                pH = [ph.ps(f"pH{n}", [P, up * FC, P]) for n in range(2)]
                pY = [ph.ps(f"pY{n}", [P, D]) for n in range(2)]
                xs_loaded = [ph.sem(f"xs_loaded{n}") for n in range(UN)]
                w1_loaded = [ph.sem(f"w1_loaded{n}") for n in range(UN)]
                w2_loaded = [ph.sem(f"w2_loaded{n}") for n in range(UN)]
                y_stored = [ph.sem(f"y_stored{n}") for n in range(UN)]
                idx_ready, to_ready = ph.sem("idx_ready"), ph.sem("to_ready")
                turned, xsT_ready = ph.sem("turned"), ph.sem("xsT_ready")
                h_summed, h_gated, h_ready = ph.sem("h_summed"), ph.sem("h_gated"), ph.sem("h_ready")
                y_summed, y_ready, last_stored = ph.sem("y_summed"), ph.sem("y_ready"), ph.sem("last_stored")
                combine_load, combine_rstds, combine_add = combine(ph, shared, post_norm, final, w1)
                block = ph.block()
                w1_v, w2_v = A[w1_name], A[w2_name]
                W2_INC = 32 if b2_name else 16

                def loop(eng, step):
                    further = eng.value_load(more[0:1, 0:1], min_val=LEAST - 2, max_val=T // UN - 2)
                    for i in range(2):
                        for b in range(UN):
                            step(i, b)
                    with eng.Fori(2, T // UN) as i:
                        with eng.If(i < further + 2):
                            for b in range(UN):
                                step(i, b)
                    return further + 1

                def before(i, b, by):
                    return i + (b - by) // UN, (b - by) % UN

                def early(i, b, n):
                    return isinstance(i, int) and UN * i + b < n

                @block.sync
                def _(sp):
                    def step(i, b):
                        t = UN * i + b
                        e = sp.value_load(etab[0:1, bass.ds(t, 1)], min_val=0, max_val=EN - 1)
                        other = {}
                        if not early(i, b, UN):
                            sp.wait_ge(y_ready, t - UN + 1)
                            held = sp.value_load(etab[0:1, bass.ds(t - UN, 1)], min_val=0, max_val=EN - 1)
                            other = {"cond": e != held}
                        sp.dma_start(w1[b][:, :], w1_v[bass.ds(e, 1), :, :].rearrange("a p c -> (a p) c"), **other)\
                            .then_inc(w1_loaded[b], 16)
                        sp.dma_start(w2[b][:, :], w2_v[bass.ds(e, 1), :, :].rearrange("a p c -> (a p) c"), **other)\
                            .then_inc(w2_loaded[b], 16)
                        if b2_name:
                            sp.dma_start(b2[b][:, :], A[b2_name][bass.ds(e, 1), :].to_broadcast([P, D]), **other)\
                                .then_inc(w2_loaded[b], 16)
                    loop(sp, step)
                    sp.wait_ge(last_stored, 16 * UN)
                    combine_load(sp)

                @block.gpsimd
                def _(pool):
                    def store(i, b, signal):
                        t = UN * i + b
                        pool.wait_ge(y_ready, t + 1)
                        nc.gpsimd.tensor_copy(to[b][:, :], dest[:, bass.ds(t, 1)]).then_inc(to_ready, 1)
                        pool.wait_ge(to_ready, t + 1)
                        pool.nop(nofuse=True)
                        pool.indirect_dma_start(out=y_rows[:, :], in_=ys[b][:, :], in_offset=None,
                                                out_offset=bass.IndirectOffsetOnAxis(ap=to[b][:, :], axis=0))\
                            .then_inc(signal, 16)

                    def load(i, b):
                        t = UN * i + b
                        if not early(i, b, UN):
                            pool.wait_ge(turned, t - UN + 1)
                            pool.wait_ge(xs_loaded[b], 16 * i)
                        if isinstance(i, int) and t < first:
                            pool.dma_start(xs[b][:, :], xn_rows[t * P:(t + 1) * P, :]).then_inc(xs_loaded[b], 16)
                            return
                        nc.gpsimd.tensor_copy(idx[b][:, :], table[:, bass.ds(t - first, 1)]).then_inc(idx_ready, 1)
                        pool.wait_ge(idx_ready, t - first + 1)
                        pool.nop(nofuse=True)
                        pool.indirect_dma_start(out=xs[b][:, :], out_offset=None, in_=xn_rows[:, :],
                                                in_offset=bass.IndirectOffsetOnAxis(ap=idx[b][:, :], axis=0))\
                            .then_inc(xs_loaded[b], 16)

                    def step(i, b):
                        load(i, b)
                        if not early(i, b, UN + 1):
                            store(*before(i, b, UN + 1), y_stored[(b - 1) % UN])
                    last = loop(pool, step)
                    store(last - 1, UN - 1, y_stored[UN - 1])
                    for b in range(UN):
                        store(last, b, last_stored)
                    combine_rstds(pool)

                @block.tensor
                def _(pe):
                    def turn(i, b):
                        t = UN * i + b
                        pe.wait_ge(xs_loaded[b], 16 * (i + 1))
                        if not early(i, b, 2):
                            pe.wait_ge(xsT_ready, t - 1)
                        for c in range(DC):
                            ins = nc.tensor.transpose(pT[b % 2][:, c, :], xs[b][:, c * P:(c + 1) * P], ident[:, :])
                        ins.then_inc(turned, 1)

                    def rise(i, b):
                        t = UN * i + b
                        pe.wait_ge(w1_loaded[b], 16 * (i + 1))
                        pe.wait_ge(xsT_ready, t + 1)
                        if not early(i, b, 2):
                            pe.wait_ge(h_ready, t - 1)
                        for f in range(up * FC):
                            for c in range(DC):
                                at = (f // FC * DC + c) * F + f % FC * P
                                ins = nc.tensor.matmul(pH[b % 2][:, f, :], w1[b][:, at:at + P], xsT[b % 2][:, c, :],
                                                       start=(c == 0), stop=(c == DC - 1))
                        ins.then_inc(h_summed, 1)

                    def fall(i, b):
                        t = UN * i + b
                        pe.wait_ge(w2_split, t + 1)
                        pe.wait_ge(h_split, t + 1)
                        if not early(i, b, 2):
                            pe.wait_ge(y_ready, t - 1)
                        m = b % 2
                        for f in range(FC):
                            for n, (h, w) in enumerate(((h_hi, w2_hi), (h_hi, w2_lo), (h_lo, w2_hi))):
                                ins = nc.tensor.matmul(pY[m][:, :], h[m][:, f, :], w[m][:, f * D:(f + 1) * D],
                                                       start=(f == 0 and n == 0), stop=(f == FC - 1 and n == 2))
                        ins.then_inc(y_summed, 1)

                    def step(i, b):
                        turn(i, b)
                        if not early(i, b, 1):
                            rise(*before(i, b, 1))
                        if not early(i, b, 2):
                            fall(*before(i, b, 2))
                    last = loop(pe, step)
                    rise(last, UN - 1)
                    fall(last, UN - 2)
                    fall(last, UN - 1)

                @block.scalar
                def _(act):
                    def step(i, b):
                        t = UN * i + b
                        act.wait_ge(w2_loaded[b], W2_INC * (i + 1))
                        if not early(i, b, 2):
                            act.wait_ge(y_summed, t - 1)
                        nc.scalar.activation(w2_hi[b % 2][:, :], w2[b][:, :], ACT.Copy).then_inc(w2_rounded, 1)
                        act.wait_ge(h_summed, t + 1)
                        if kind == "silu":
                            if not early(i, b, 2):
                                act.wait_ge(h_ready, t - 1)
                            nc.scalar.activation(sg[b % 2][:, :, :], pH[b % 2][:, 0:FC, :], ACT.Silu)\
                                .then_inc(h_gated, 1)
                        else:
                            if not early(i, b, 2):
                                act.wait_ge(h_split, t - 1)
                            for f in range(FC):
                                b1 = w1[b][:, DC * F + f:DC * F + f + 1]
                                ins = nc.scalar.activation(hT[b % 2][:, f, :], pH[b % 2][:, f, :],
                                                           ACT.Relu if kind == "relu" else ACT.Gelu, bias=b1)
                            ins.then_inc(h_ready, 1)
                        act.wait_ge(h_ready, t + 1)
                        nc.scalar.activation(h_hi[b % 2][:, :, :], hT[b % 2], ACT.Copy).then_inc(h_rounded, 1)
                    loop(act, step)

                @block.vector
                def _(dve):
                    def copy(i, b):
                        t = UN * i + b
                        dve.wait_ge(turned, t + 1)
                        if not early(i, b, 2):
                            dve.wait_ge(h_summed, t - 1)
                        nc.vector.tensor_copy(xsT[b % 2][:, :, :], pT[b % 2][:, :, :]).then_inc(xsT_ready, 1)

                    def product(i, b):
                        t = UN * i + b
                        dve.wait_ge(h_gated, t + 1)
                        if not early(i, b, 2):
                            dve.wait_ge(h_split, t - 1)
                        nc.vector.tensor_tensor(hT[b % 2], sg[b % 2][:, :, :], pH[b % 2][:, FC:2 * FC, :],
                                                ALU.mult).then_inc(h_ready, 1)

                    def split_w2(i, b):
                        dve.wait_ge(w2_rounded, UN * i + b + 1)
                        nc.vector.tensor_tensor(w2_lo[b % 2][:, :], w2[b][:, :], w2_hi[b % 2][:, :].bitcast(F32),
                                                ALU.subtract).then_inc(w2_split, 1)

                    def split_h(i, b):
                        dve.wait_ge(h_rounded, UN * i + b + 1)
                        nc.vector.tensor_tensor(h_lo[b % 2][:, :, :], hT[b % 2], h_hi[b % 2][:, :, :].bitcast(F32),
                                                ALU.subtract).then_inc(h_split, 1)

                    def end(i, b):
                        t = UN * i + b
                        dve.wait_ge(y_summed, t + 1)
                        if not early(i, b, UN):
                            dve.wait_ge(y_stored[b], 16 * i)
                        if b2_name:
                            ins = nc.vector.tensor_tensor(ys[b][:, :], pY[b % 2][:, :], b2[b][:, :], ALU.add)
                        else:
                            ins = nc.vector.tensor_copy(ys[b][:, :], pY[b % 2][:, :])
                        ins.then_inc(y_ready, 1)

                    def step(i, b):
                        copy(i, b)
                        if not early(i, b, 1):
                            split_w2(*before(i, b, 1))
                            if kind == "silu":
                                product(*before(i, b, 1))
                            split_h(*before(i, b, 1))
                        if not early(i, b, 2):
                            end(*before(i, b, 2))
                    last = loop(dve, step)
                    split_w2(last, UN - 1)
                    if kind == "silu":
                        product(last, UN - 1)
                    split_h(last, UN - 1)
                    end(last, UN - 2)
                    end(last, UN - 1)
                    combine_add(dve)

        def early_out():
            with Phase("early") as ph:
                stored = ph.sem("stored")
                block = ph.block()

                @block.sync
                def _(sp):
                    sp.dma_start(out.rearrange("(t p) d -> p t d", p=P), x[:, :, :]).then_inc(stored, 16)
                    sp.wait_ge(stored, 16)

        def ffn(L, E, F, kind, gw, gb, b2=True, all_probs=False, shared=0, post_norm=False, final=False):
            gate(L, E, gw, gb, all_probs, shared)
            experts(L, E, F, kind, shared, f"w1_{L}", f"w2_{L}", f"b2_{L}" if b2 else None,
                    post_norm, final)

        halves = [graph0,
                  lambda: ffn(0, 16, 512, "relu", "L0_ffn_gate_w", "L0_ffn_gate_b", post_norm=True),
                  graph1,
                  lambda: ffn(1, 8, 512, "gelu", "L1_ffn_gate_w", "L1_ffn_gate_b", all_probs=True),
                  graph2,
                  lambda: ffn(2, 8, 1024, "gelu", "L2_ffn_Wr", None, shared=1),
                  graph3,
                  lambda: ffn(3, 16, 512, "silu", "L3_ffn_gate_w", "L3_ffn_gate_b", b2=False, final=True)]
        for n, half in enumerate(halves[:stop]):
            half()
            if n % 2 == 1:
                nc.clear_and_free_semaphores(sems)
                sems.clear()
                nc.all_engine_barrier()
        if stop < len(halves):
            early_out()


def _arrays(inputs):
    import numpy as np

    def a(n):
        return np.asarray(inputs[n])

    def rows(w):
        e, k, f = w.shape
        return w.reshape(e, k // P, P, f).transpose(0, 2, 1, 3).reshape(e, P, k // P * f)

    def cols(b):
        return b.reshape(b.shape[0], -1, P).transpose(0, 2, 1)

    out = {n: a(n) for n in inputs if not n.split("_", 1)[-1].startswith("ffn")}
    for n in ("L0_ffn_gate_w", "L0_ffn_gate_b", "L0_ffn_gamma", "L0_ffn_beta", "L1_ffn_gate_w", "L1_ffn_gate_b",
              "L2_ffn_Wr", "L3_ffn_gate_w", "L3_ffn_gate_b"):
        out[n] = a(n)
    out["adjT"] = a("adj").T
    out["neighT"] = out.pop("L0_gnn_neigh").T
    out["L1_gnn_WT"] = out.pop("L1_gnn_W").T
    out["L3_gnn_aT"] = out.pop("L3_gnn_a").reshape(-1, P).T
    out["w1_0"] = np.concatenate([rows(a("L0_ffn_w1")), cols(a("L0_ffn_b1"))], 2)
    out["w2_0"], out["b2_0"] = rows(a("L0_ffn_w2")), a("L0_ffn_b2")
    out["w1_1"] = np.concatenate([rows(a("L1_ffn_W1")), cols(a("L1_ffn_b1"))], 2)
    out["w2_1"], out["b2_1"] = rows(a("L1_ffn_W2")), a("L1_ffn_b2")
    w1 = np.concatenate([a("L2_ffn_W1p"), a("L2_ffn_W1s")[None]])
    w2 = np.concatenate([a("L2_ffn_W2p"), a("L2_ffn_W2s")[None]])
    out["w1_2"] = np.concatenate([rows(w1), cols(np.concatenate([a("L2_ffn_b1p"), a("L2_ffn_b1s")[None]]))], 2)
    out["w2_2"], out["b2_2"] = rows(w2), np.concatenate([a("L2_ffn_b2p"), a("L2_ffn_b2s")[None]])
    out["w1_3"] = np.concatenate([rows(a("L3_ffn_w1")), rows(a("L3_ffn_w2"))], 2)
    out["w2_3"] = rows(a("L3_ffn_w3"))
    return {n: np.ascontiguousarray(v) for n, v in out.items()}


STOP = 99


def kernel(**inputs):
    import numpy as np
    import concourse.bacc as bacc
    from concourse.bass_utils import run_bass_kernel_spmd

    nc = bacc.Bacc("TRN2", target_bir_lowering=False, num_devices=1)
    arrays = _arrays(inputs)
    A = {n: nc.dram_tensor(n + "_in", v.shape, mybir.dt.from_np(v.dtype), kind="ExternalInput").ap()
         for n, v in arrays.items()}
    out = nc.dram_tensor("out", [N, D], mybir.dt.float32, kind="ExternalOutput").ap()
    build(nc, A, out, STOP)
    r = run_bass_kernel_spmd(nc, [{n + "_in": v for n, v in arrays.items()}], core_ids=[0])
    return np.asarray(r.results[0]["out"])
```
